# Optimizing a Trainium2 kernel written in Bass

```python
import numpy as np
import jax
import jax.numpy as jnp

def _softmax(x, axis=-1):
    return jax.nn.softmax(x, axis=axis)

def _gelu(x):
    return jax.nn.gelu(x, approximate=True)

def _silu(x):
    return jax.nn.silu(x)

def _sigmoid(x):
    return jax.nn.sigmoid(x)

def _layernorm(x, axis=-1, eps=1e-05):
    m = jnp.mean(x, axis=axis, keepdims=True)
    v = jnp.var(x, axis=axis, keepdims=True)
    return (x - m) / jnp.sqrt(v + eps)

def _scatter_add(tgt, idx, src, axis=0):
    return tgt.at[idx].add(src)

def _segment_sum(src, seg, n):
    return jax.ops.segment_sum(src, seg, n)
kernel_name = 'mk_seq_preln_d1_jaxref_r8_1d0f19'

def setup_inputs(seed: int=0):
    np.random.seed(seed)
    _w = jnp.asarray

    def _L0_attn_setup():
        import jax, jax.numpy as jnp
        import numpy as np
        B, T, D, H = (2, 256, 128, 16)
        DH = D // H
        ROPE_BASE = 10000.0

        def _rope(Xh, cos, sin):
            x0 = Xh[..., 0::2]
            x1 = Xh[..., 1::2]
            r0 = cos * x0 - sin * x1
            r1 = sin * x0 + cos * x1
            return jnp.stack((r0, r1), axis=-1).reshape(Xh.shape)
        key = jax.random.key(seed)
        ks = jax.random.split(key, 5)
        s = 1.0 / np.sqrt(D)
        return {'X': jax.random.normal(ks[0], (B, T, D), dtype=jnp.float32), 'W_q': jax.random.normal(ks[1], (D, D), dtype=jnp.float32) * s, 'W_k': jax.random.normal(ks[2], (D, D), dtype=jnp.float32) * s, 'W_v': jax.random.normal(ks[3], (D, D), dtype=jnp.float32) * s, 'W_o': jax.random.normal(ks[4], (D, D), dtype=jnp.float32) * s}
    _L0_attn_in = _L0_attn_setup()

    def _L0_ffn_setup():
        import jax, jax.numpy as jnp
        import numpy as np
        DIM = 128
        HIDDEN = 384
        SCALE = 1.0 / 127.0

        def _dequant(w_int, dtype):
            return w_int.astype(dtype) * jnp.asarray(SCALE, dtype)
        key = jax.random.key(seed)
        k_x, k_g, k_u, k_d = jax.random.split(key, 4)
        x = jax.random.normal(k_x, (4, 256, DIM), dtype=jnp.float32)
        w_gate = jax.random.randint(k_g, (HIDDEN, DIM), -127, 128, dtype=jnp.int32)
        w_up = jax.random.randint(k_u, (HIDDEN, DIM), -127, 128, dtype=jnp.int32)
        w_down = jax.random.randint(k_d, (DIM, HIDDEN), -127, 128, dtype=jnp.int32)
        return {'x': x, 'w_gate': w_gate, 'w_up': w_up, 'w_down': w_down}
    _L0_ffn_in = _L0_ffn_setup()
    _d = {'L0_attn_X': _L0_attn_in['X'], 'L0_attn_W_q': _L0_attn_in['W_q'], 'L0_attn_W_k': _L0_attn_in['W_k'], 'L0_attn_W_v': _L0_attn_in['W_v'], 'L0_attn_W_o': _L0_attn_in['W_o'], 'L0_ffn_w_gate': _L0_ffn_in['w_gate'], 'L0_ffn_w_up': _L0_ffn_in['w_up'], 'L0_ffn_w_down': _L0_ffn_in['w_down']}
    _x0 = _d['L0_attn_X']
    _d['L0_attn_X'] = jax.random.normal(jax.random.fold_in(jax.random.key(seed), 1), (4, 512, 128), dtype=_x0.dtype)
    del _x0
    return _d

def reference(L0_attn_X, L0_attn_W_q, L0_attn_W_k, L0_attn_W_v, L0_attn_W_o, L0_ffn_w_gate, L0_ffn_w_up, L0_ffn_w_down):

    def _L0_attn_ref(X, W_q, W_k, W_v, W_o):
        import jax, jax.numpy as jnp
        import numpy as np
        B, T, D, H = (2, 256, 128, 16)
        DH = D // H
        ROPE_BASE = 10000.0

        def _rope(Xh, cos, sin):
            x0 = Xh[..., 0::2]
            x1 = Xh[..., 1::2]
            r0 = cos * x0 - sin * x1
            r1 = sin * x0 + cos * x1
            return jnp.stack((r0, r1), axis=-1).reshape(Xh.shape)
        b, t, d = X.shape
        Q = X @ W_q.T
        K = X @ W_k.T
        V = X @ W_v.T
        Qh = Q.reshape(b, t, H, DH).transpose(0, 2, 1, 3)
        Kh = K.reshape(b, t, H, DH).transpose(0, 2, 1, 3)
        Vh = V.reshape(b, t, H, DH).transpose(0, 2, 1, 3)
        theta = ROPE_BASE ** (-2.0 * jnp.arange(DH // 2, dtype=jnp.float32) / DH)
        pos = jnp.arange(t, dtype=jnp.float32)
        angles = pos[:, None] * theta[None, :]
        cos = jnp.cos(angles).astype(Qh.dtype)
        sin = jnp.sin(angles).astype(Qh.dtype)
        Qr = _rope(Qh, cos, sin)
        Kr = _rope(Kh, cos, sin)
        scores = jnp.einsum('bhqd,bhkd->bhqk', Qr, Kr) * DH ** (-0.5)
        causal = jnp.triu(jnp.ones((t, t), dtype=bool), 1)
        neg = jnp.finfo(scores.dtype).min
        scores = jnp.where(causal[None, None], neg, scores)
        pattern = jax.nn.softmax(scores, axis=-1)
        heads = jnp.einsum('bhqk,bhkd->bhqd', pattern, Vh)
        out = heads.transpose(0, 2, 1, 3).reshape(b, t, d)
        return out @ W_o.T

    def _L0_ffn_ref(x, w_gate, w_up, w_down):
        import jax, jax.numpy as jnp
        import numpy as np
        DIM = 128
        HIDDEN = 384
        SCALE = 1.0 / 127.0

        def _dequant(w_int, dtype):
            return w_int.astype(dtype) * jnp.asarray(SCALE, dtype)
        wg = _dequant(w_gate, x.dtype)
        wu = _dequant(w_up, x.dtype)
        wd = _dequant(w_down, x.dtype)
        gate = jnp.einsum('bsd,hd->bsh', x, wg)
        up = jnp.einsum('bsd,hd->bsh', x, wu)
        h = jax.nn.silu(gate) * up
        return jnp.einsum('bsh,dh->bsd', h, wd)
    x = L0_attn_X
    x = x + _L0_attn_ref(_layernorm(x, axis=-1), L0_attn_W_q, L0_attn_W_k, L0_attn_W_v, L0_attn_W_o)
    x = x + _L0_ffn_ref(_layernorm(x, axis=-1), L0_ffn_w_gate, L0_ffn_w_up, L0_ffn_w_down)
    return x

_drawn_inputs = setup_inputs


def setup_inputs(seed=0):
    import zlib

    import numpy as np

    out = dict(_drawn_inputs(seed))
    spreads = {}
    factors = {}
    for name, (base, spread) in spreads.items():
        noise = np.random.default_rng([zlib.crc32(name.encode()), seed]).standard_normal(out[name].shape)
        drawn = base * np.exp(spread * noise) if base else spread * noise
        out[name] = jnp.asarray(drawn.astype(out[name].dtype))
    for name, factor in factors.items():
        out[name] = (out[name] * factor).astype(out[name].dtype)
    return out
```

```python
from contextlib import ExitStack

import concourse.bass as bass
from concourse import mybir

B, T, D = 4, 512, 128
H, DH = 16, 8
P = 128
NB = T // P
HID = 384
NC = HID // P
UH = 4
G = H // UH
EPS = 1e-5
SCALE = float(DH) ** -0.5
W_SCALE = 1.0 / 127.0
MASKED = -1e30

Q_PART = [0, 0, 0, 1, 1, 2]
K_PART = [0, 1, 2, 0, 1, 0]
TERMS = len(Q_PART)
XR = TERMS * DH
MR = 3

NAT = [(3, a, 1) for a in range(4)] + [(2, a, 1) for a in range(4)] + [(1, 0, 2), (1, 2, 2), (0, 0, 4)]
STS = ([[(a, 0, 0)] for a in range(4)] + [[(a, 1, 0), (a, 3, 384)] for a in range(4)]
       + [[(2 * p, 2, 0), (2 * p + 1, 2, 256)] for p in range(2)])
PLACE = {(a, kb): (n, c) for n, pieces in enumerate(STS) for a, kb, c in pieces}
NN, NS = len(NAT), len(STS)
POS = 14
ST_AT = 4
PV_AT = {3: 0, 5: 1, 7: 3, 9: 2}


def layer_kernel(nc, X_d, WqT, WqsT, WkT, WksT, WvT, WoT, WgT, WuT, WdT, cos_d, sin_d, ident_d, mask_d, out_d):
    F32, BF16, I32 = mybir.dt.float32, mybir.dt.bfloat16, mybir.dt.int32
    ALU, ACT, AX = mybir.AluOpType, mybir.ActivationFunctionType, mybir.AxisListType

    x_v = X_d.rearrange("b (i p) d -> b p i d", p=P)
    out_v = out_d.rearrange("b (i p) d -> b p i d", p=P)
    q_scr = nc.dram_tensor("q_scr", [B, XR + MR, H, T], BF16, kind="Internal").ap()
    k_scr = nc.dram_tensor("k_scr", [B, XR, H, T], BF16, kind="Internal").ap()

    ctx = ExitStack()
    with ctx:
        def sb(name, shape, dt=F32):
            return ctx.enter_context(nc.sbuf_tensor(name, shape, dt))

        def sem(name):
            return ctx.enter_context(nc.semaphore(name))

        def bank(name):
            return ctx.enter_context(nc.psum_tensor(name, [P, T], F32))

        x_sb = sb("x_sb", [P, B * NB, D])
        w_proj = sb("w_proj", [P, 6, D])
        w_int = sb("w_int", [P, 3, HID], I32)
        w_ffn = sb("w_ffn", [P, 3, HID])
        cos, sin = sb("cos", [P, T]), sb("sin", [P, T])
        ident, ident16 = sb("ident", [P, P]), sb("ident16", [P, P], BF16)
        mask, mask16 = sb("mask", [P, P]), sb("mask16", [P, P], BF16)
        minus = sb("minus", [P, T], BF16)
        qx, kx = sb("qx", [P, H, T], BF16), sb("kx", [P, H, T], BF16)
        stats, mean_var, rstd = sb("stats", [P, NB, 6]), sb("mean_var", [P, NB, 2]), sb("rstd", [P, NB])
        stats2, mean_var2, rstd2 = sb("stats2", [P, NB, 6]), sb("mean_var2", [P, NB, 2]), sb("rstd2", [P, NB])
        power = sb("power", [P, NB])
        xn, xnT = sb("xn", [P, NB, D]), sb("xnT", [P, T])
        rot = sb("rot", [P, 4, T])
        rest = sb("rest", [P, 2, T])
        parts = sb("parts", [P, 2, 3, T], BF16)
        v_nat = sb("v_nat", [P, NB, D])
        v_aug = sb("v_aug", [P, NB, H, 32])
        m_row = sb("m_row", [P, UH * NB])
        m_rest = sb("m_rest", [P, UH * NB])
        m_parts = sb("m_parts", [P, 3, UH * NB], BF16)
        mT = sb("mT", [3 * UH * NB, P], BF16)
        pT = sb("pT", [P, 2, NS, T])
        o_sb = sb("o_sb", [P, 2, T])
        denom = sb("denom", [P, NB, 8])
        o_nat, oT = sb("o_nat", [P, NB, D]), sb("oT", [P, T])
        x2, xn2, xn2T = sb("x2", [P, NB, D]), sb("xn2", [P, NB, D]), sb("xn2T", [P, T])
        th, gated = sb("th", [P, T]), sb("gated", [P, T])
        hT = sb("hT", [P, NC, T])

        nat_b = [bank("nat0"), bank("nat1")]
        st_b = [bank("st0"), bank("st1")]
        o_b = [bank("o0"), bank("o1")]
        m_b = [bank("misc0"), bank("misc1")]

        x0_in, x_in, w_in, wi_in = sem("x0_in"), sem("x_in"), sem("w_in"), sem("wi_in")
        c_in, zero_w = sem("c_in"), sem("zero_w")
        ones_in, scr_q, scr_k = sem("ones_in"), sem("scr_q"), sem("scr_k")
        pair_in = [sem("pair0_in"), sem("pair1_in")]
        m_in = [sem("m_in0"), sem("m_in1")]
        stored = sem("stored")
        nat_done, st_done, pv_done, mt_done = sem("nat_done"), sem("st_done"), sem("pv_done"), sem("mt_done")
        xt_done, proj_done, ot_done, ont_done = sem("xt_done"), sem("proj_done"), sem("ot_done"), sem("ont_done")
        wo_done, x2t_done, gu_done, down_done = sem("wo_done"), sem("x2t_done"), sem("gu_done"), sem("down_done")
        max_done, rot_done, const_done = sem("max_done"), sem("rot_done"), sem("const_done")
        ln1, ln2, xn_done, xn2_done = sem("ln1"), sem("ln2"), sem("xn_done"), sem("xn2_done")
        denom_done, onat_done, x2_done = sem("denom_done"), sem("onat_done"), sem("x2_done")
        gated_done, h_done, y_done = sem("gated_done"), sem("h_done"), sem("y_done")
        exp_done, mtc_done, xtc_done, vc_done = sem("exp_done"), sem("mtc_done"), sem("xtc_done"), sem("vc_done")
        oc_done, ontc_done, x2tc_done, tanh_done = sem("oc_done"), sem("ontc_done"), sem("x2tc_done"), sem("tanh_done")
        clear_done, mp, mask_done = sem("clear_done"), sem("mp"), sem("mask_done")
        split, va_done, rs1_done, rs2_done = sem("split"), sem("va_done"), sem("rs1_done"), sem("rs2_done")
        MASKS = 5
        MP, SPLIT = 4, 5

        block = ctx.enter_context(nc.Block())

        @block.tensor
        def _(pe):
            def nat_step(u, g, i):
                j, a0, n = NAT[i]
                w = P * (j + 1)
                out = nat_b[(i + g * NN) % 2]
                pe.wait_ge(max_done, u * NN + i - 1) if not (isinstance(u, int) and u * NN + i < 2) else None
                o3 = out[:, 0:n * w].rearrange("p (a k) -> p a k", a=n)
                pe.matmul(o3[:, :, P * j:w], ident16[:, :],
                          mask16[:, :].unsqueeze(1).broadcast_to([P, n, P]) if n > 1 else mask16[:, :].unsqueeze(1),
                          start=True, stop=False, skip_group_check=True)
                for a in range(n):
                    h = UH * g + a0 + a
                    mm = pe.matmul(o3[:, a, :], qx[:, h, P * j:P * j + P], kx[:, h, 0:w],
                                   start=False, stop=True, skip_group_check=True)
                mm.then_inc(nat_done, 1)

            def st_step(u, b, g, i):
                if i == 0:
                    pe.wait_ge(m_in[g % 2], 16 * (G // 2 * b + g // 2 + 1))
                if not (isinstance(u, int) and u * NS + i < 2):
                    pe.wait_ge(exp_done, u * NS + i - 1)
                for a, kb, c in STS[i]:
                    h = UH * g + a
                    mm = pe.matmul(st_b[i % 2][:, c:c + T - P * kb], kx[:, h, P * kb:P * kb + P],
                                   qx[:, h, P * kb:T], start=True, stop=True)
                mm.then_inc(st_done, 1)

            def pv_step(u, g, kb, b, first):
                need = {0: 1, 1: 3, 3: 3, 2: 5}[kb]
                pe.wait_ge(mask_done, u * MASKS + need)
                if kb == 0 and g == 0:
                    pe.wait_ge(va_done, b + 1)
                if kb == 0 and g % 2 == 0 and not first:
                    pe.wait_ge(oc_done, 2 * b + g // 2 - 1)
                for a in range(UH):
                    n, c = PLACE[a, kb]
                    mm = pe.matmul(o_b[g // 2][32 * a:32 * a + 32, P * kb:T], v_aug[:, kb, UH * g + a, :],
                                   pT[:, g % 2, n, c:c + T - P * kb],
                                   start=(g % 2 == 0 and kb == 0), stop=(g % 2 == 1 and kb == 2),
                                   skip_group_check=True)
                if kb == 2:
                    mm.then_inc(pv_done, 1)

            def max_T(u):
                n = MP * (u + 1) if isinstance(u, int) else pe.to_reg(MP * (u + 1))
                pe.wait_ge(const_done, 1)
                pe.wait_ge(mp, n)
                pe.transpose(m_b[0][0:3 * UH * NB, 0:P // 2].bitcast(BF16),
                             m_parts[:, :, :].rearrange("p c m -> p (c m)"), ident16[:, :]).then_inc(mt_done, 1)

            def four_T(out, src, done):
                for i in range(NB):
                    mm = pe.transpose(out[:, P * i:P * i + P], src(i), ident[:, :])
                mm.then_inc(done, 1)

            def xn_T(b):
                pe.wait_ge(xn_done, b + 1)
                four_T(m_b[1], lambda i: xn[:, i, :], xt_done)

            def project(b, n):
                if n == 0:
                    pe.wait_ge(xtc_done, b + 1)
                if n < 4:
                    pe.matmul(m_b[n % 2][:, :], w_proj[:, n, :], xnT[:, :], start=True, stop=True).then_inc(proj_done, 1)
                else:
                    for i in range(NB):
                        mm = pe.matmul(m_b[0][:, P * i:P * i + P], xnT[:, P * i:P * i + P], w_proj[:, 4, :],
                                       start=True, stop=True)
                    mm.then_inc(proj_done, 1)

            def o_T(b, t):
                pe.wait_ge(oc_done, 2 * b + t + 1)
                four_T(m_b[1], lambda i: o_sb[:, t, P * i:P * i + P], ot_done)

            def on_T(b):
                pe.wait_ge(onat_done, 2 * b + 2)
                four_T(m_b[0], lambda i: o_nat[:, i, :], ont_done)

            def w_o(b):
                pe.wait_ge(ontc_done, b + 1)
                for i in range(NB):
                    mm = pe.matmul(m_b[1][:, P * i:P * i + P], oT[:, P * i:P * i + P], w_proj[:, 5, :],
                                   start=True, stop=True)
                mm.then_inc(wo_done, 1)

            def xn2_T(b):
                pe.wait_ge(xn2_done, b + 1)
                four_T(m_b[1], lambda i: xn2[:, i, :], x2t_done)

            def gate_up(b, c):
                if c == 0:
                    pe.wait_ge(x2tc_done, b + 1)
                else:
                    pe.wait_ge(h_done, NC * b + c)
                for n in range(2):
                    pe.matmul(m_b[n][:, :], w_ffn[:, n, P * c:P * c + P], xn2T[:, :],
                              start=True, stop=True).then_inc(gu_done, 1)

            def down(b):
                pe.wait_ge(h_done, NC * b + NC)
                for i in range(NB):
                    for c in range(NC):
                        mm = pe.matmul(m_b[0][:, P * i:P * i + P], hT[:, c, P * i:P * i + P],
                                       w_ffn[:, 2, P * c:P * c + P], start=(c == 0), stop=(c == NC - 1))
                mm.then_inc(down_done, 1)

            def body(b, first, last):
                for g in range(G):
                    u = b * G + g
                    for p in range(POS):
                        if p < NN and not (last and g == G - 1):
                            ng = (g + 1) % G
                            nb_ = b + 1 if g == G - 1 else b
                            if p == 0 and ng % 2 == 0:
                                pe.wait_ge(pair_in[ng // 2], 32 * (nb_ + 1))
                            nat_step(u + 1, ng, p)
                        if p in PV_AT and not (first and g == 0):
                            pv_step(u - 1, (g - 1) % G, PV_AT[p], b - 1 if g == 0 else b,
                                    first if g else False)
                        if p == 1:
                            if g == 0 and not first:
                                pe.wait_ge(mtc_done, u)
                            if g == 1 and not last:
                                pe.wait_ge(rot_done, 4 * (b + 1) + 3)
                            if g == 1 and last:
                                pe.wait_ge(mtc_done, u)
                            if g == 2 and not last:
                                pe.wait_ge(vc_done, b + 2)
                            if g == 2 and last:
                                pe.wait_ge(ontc_done, b)
                            if g == 3 and not first:
                                pe.wait_ge(h_done, NC * (b - 1) + 2)
                            if g == 3 and first:
                                pe.wait_ge(mtc_done, u)
                            max_T(u)
                        if g == 0 and not last:
                            if p == 3:
                                xn_T(b + 1)
                            if p == 5:
                                pe.wait_ge(mtc_done, u + 1)
                                project(b + 1, 0)
                            if p == 6:
                                project(b + 1, 1)
                            if p == 8:
                                pe.wait_ge(rot_done, 4 * (b + 1) + 1)
                                project(b + 1, 2)
                            if p == 9:
                                pe.wait_ge(rot_done, 4 * (b + 1) + 2)
                                project(b + 1, 3)
                        if g == 0 and not first and p == 12:
                            if last:
                                pe.wait_ge(h_done, NC * (b - 1))
                            else:
                                pe.wait_ge(rot_done, 4 * (b + 1) + 4)
                            o_T(b - 1, 0)
                        if g == 1 and not first:
                            if p == 3:
                                pe.wait_ge(onat_done, 2 * (b - 1) + 1)
                                o_T(b - 1, 1)
                            if p == 6:
                                pe.wait_ge(mtc_done, u + 1)
                                on_T(b - 1)
                            if p == 9:
                                w_o(b - 1)
                        if g == 1 and not last and p == 11:
                            if first:
                                pe.wait_ge(mtc_done, u + 1)
                            else:
                                pe.wait_ge(ontc_done, b)
                            project(b + 1, 4)
                        if g == 2 and not first:
                            if p == 4:
                                xn2_T(b - 1)
                            if p == 6:
                                pe.wait_ge(mtc_done, u + 1)
                                gate_up(b - 1, 0)
                            if p == 10:
                                gate_up(b - 1, 1)
                        if g == 3 and not first:
                            if p == 4:
                                pe.wait_ge(mtc_done, u + 1)
                                gate_up(b - 1, 2)
                            if p == 9:
                                down(b - 1)
                        if p >= ST_AT:
                            st_step(u, b, g, p - ST_AT)

            pe.wait_ge(const_done, 2)
            xn_T(0)
            pe.wait_ge(w_in, 16 * 6)
            project(0, 0)
            project(0, 1)
            pe.wait_ge(rot_done, 1)
            project(0, 2)
            pe.wait_ge(rot_done, 2)
            project(0, 3)
            pe.wait_ge(rot_done, 3)
            project(0, 4)
            pe.wait_ge(ones_in, 32)
            pe.wait_ge(pair_in[0], 32)
            for i in range(NN):
                nat_step(0, 0, i)
            pe.wait_ge(vc_done, 1)
            pe.wait_ge(rot_done, 4)
            pe.wait_ge(const_done, 3)
            body(0, True, False)
            with pe.Fori(1, B - 1) as b:
                body(b, False, False)
            body(B - 1, False, True)
            for kb in (0, 1, 3, 2):
                pv_step(B * G - 1, G - 1, kb, B - 1, False)
            pe.wait_ge(h_done, NC * (B - 1))
            o_T(B - 1, 0)
            pe.wait_ge(onat_done, 2 * B - 1)
            o_T(B - 1, 1)
            pe.wait_ge(y_done, B - 1)
            on_T(B - 1)
            w_o(B - 1)
            xn2_T(B - 1)
            for c in range(NC):
                gate_up(B - 1, c)
            down(B - 1)

        @block.vector
        def _(dve):
            def row_max(u, g, i):
                j, a0, n = NAT[i]
                w = P * (j + 1)
                dve.wait_ge(nat_done, u * NN + i + 1)
                if i == 0 and not (isinstance(u, int) and u == 0):
                    dve.wait_ge(mp, MP * u)
                dve.reduce_max(m_row[:, NB * a0 + j:NB * (a0 + n - 1) + j + 1:NB],
                               nat_b[(i + g * NN) % 2][:, 0:n * w].rearrange("p (a k) -> p a k", a=n),
                               AX.X).then_inc(max_done, 1)

            def moments(b, src, st, mv, step):
                for i in range(NB):
                    last = dve.bn_stats(st[:, i, :], src(i))
                last.then_inc(step, 1)
                n = 2 * b + 1 if isinstance(b, int) else dve.to_reg(2 * b + 1)
                dve.wait_ge(x0_in, 16)
                dve.wait_ge(step, n)
                for i in range(NB):
                    last = dve.bn_aggr(mv[:, i, :], st[:, i, :])
                last.then_inc(step, 1)

            def centre(b, src, mv, rs, dst, rstd_done, done):
                dve.wait_ge(rstd_done, 2 * b + 2)
                for i in range(NB):
                    last = dve.tensor_scalar(dst[:, i, :], src(i), mv[:, i, 0:1], rs[:, i:i + 1],
                                             ALU.subtract, ALU.mult)
                last.then_inc(done, 1)

            xs = x_sb[:, :, :].rearrange("p (b i) d -> p b i d", b=B)

            def moments1(b):
                moments(b, lambda i: xs[:, b, i, :], stats, mean_var, ln1)

            def centre1(b):
                if not (isinstance(b, int) and b == 0):
                    dve.wait_ge(xt_done, b)
                centre(b, lambda i: xs[:, b, i, :], mean_var, rstd, xn, rs1_done, xn_done)

            def moments2(b):
                moments(b, lambda i: x2[:, i, :], stats2, mean_var2, ln2)

            def centre2(b):
                centre(b, lambda i: x2[:, i, :], mean_var2, rstd2, xn2, rs2_done, xn2_done)

            def rotate(b, n):
                dve.wait_ge(proj_done, 5 * b + n + 1)
                if n % 2 == 0 and not (isinstance(b, int) and b == 0):
                    dve.wait_ge(split, SPLIT * (2 * (b - 1) + n // 2) + 1)
                dve.tensor_tensor(rot[:, n, :], m_b[n % 2][:, :], (cos if n % 2 == 0 else sin)[:, :],
                                  ALU.mult).then_inc(rot_done, 1)

            def normalise(b, t):
                dve.wait_ge(ot_done, 2 * b + t + 1)
                o4 = m_b[1][:, :].rearrange("p (i a s e) -> p i a s e", i=NB, a=UH, s=2)
                dn = denom[:, :, :].rearrange("p i (a s) -> p i a s", s=2)
                dve.reciprocal(dn, o4[:, :, :, :, DH]).then_inc(denom_done, 1)
                dve.wait_ge(denom_done, 2 * b + t + 1)
                on = o_nat[:, :, :].rearrange("p i (t s a e) -> p i t s a e", t=2, s=2, a=UH)
                for s in range(2):
                    last = dve.tensor_tensor(on[:, :, t, s, :, :], o4[:, :, :, s, 0:DH],
                                             dn[:, :, :, s].unsqueeze(3).broadcast_to([P, NB, UH, DH]), ALU.mult)
                last.then_inc(onat_done, 1)

            def add_x(b):
                dve.wait_ge(wo_done, b + 1)
                xs = x_sb[:, :, :].rearrange("p (b n) d -> p b (n d)", b=B)
                dve.tensor_tensor(x2[:, :, :].rearrange("p i d -> p (i d)"), m_b[1][:, :], xs[:, b, :],
                                  ALU.add).then_inc(x2_done, 1)
                dve.wait_ge(x2_done, b + 1)

            def hidden(b, c):
                dve.wait_ge(tanh_done, NC * b + c + 1)
                dve.scalar_tensor_tensor(gated[:, :], th[:, :], 1.0, m_b[0][:, :], ALU.add,
                                         ALU.mult).then_inc(gated_done, 1)
                dve.wait_ge(gated_done, NC * b + c + 1)
                dve.wait_ge(gu_done, 2 * (NC * b + c) + 2)
                dve.scalar_tensor_tensor(hT[:, c, :], gated[:, :], 0.5, m_b[1][:, :], ALU.mult,
                                         ALU.mult).then_inc(h_done, 1)

            def add_y(b):
                dve.wait_ge(down_done, b + 1)
                x2f = x2[:, :, :].rearrange("p i d -> p (i d)")
                dve.tensor_tensor(x2f, m_b[0][:, :], x2f, ALU.add).then_inc(y_done, 1)

            def body(b, first, last):
                for g in range(G):
                    u = b * G + g
                    for p in range(POS):
                        if p < NN and not (last and g == G - 1):
                            row_max(u + 1, (g + 1) % G, p)
                        if g == 0 and not last:
                            if p == 0:
                                moments1(b + 1)
                            if p == 2:
                                centre1(b + 1)
                            if p in (5, 6, 8, 9):
                                rotate(b + 1, (5, 6, 8, 9).index(p))
                        if g == 0 and p == 12 and not first:
                            normalise(b - 1, 0)
                        if g == 1 and not first:
                            if p == 3:
                                normalise(b - 1, 1)
                            if p == 9:
                                add_x(b - 1)
                                moments2(b - 1)
                        if g == 2 and not first and p == 3:
                            centre2(b - 1)
                        if g == 2 and not first and p in (6, 10):
                            hidden(b - 1, (6, 10).index(p))
                        if g == 3 and not first:
                            if p == 4:
                                hidden(b - 1, 2)
                            if p == 9:
                                add_y(b - 1)

            dve.wait_ge(x0_in, 16)
            moments1(0)
            centre1(0)
            dve.wait_ge(c_in, 64)
            dve.tensor_copy(ident16[:, :], ident[:, :]).then_inc(const_done, 1)
            dve.tensor_copy(mask16[:, :], mask[:, :]).then_inc(const_done, 1)
            for n in range(4):
                rotate(0, n)
            dve.wait_ge(wi_in, 16 * 3)
            dve.tensor_scalar(w_ffn[:, :, :], w_int[:, :, :], W_SCALE, None, ALU.mult).then_inc(const_done, 1)
            dve.wait_ge(x_in, 16 * (B - 1))
            for i in range(NN):
                row_max(0, 0, i)
            body(0, True, False)
            with dve.Fori(1, B - 1) as b:
                body(b, False, False)
            body(B - 1, False, True)
            normalise(B - 1, 0)
            normalise(B - 1, 1)
            dve.wait_ge(stored, 16 * (B - 1))
            add_x(B - 1)
            moments2(B - 1)
            centre2(B - 1)
            for c in range(NC):
                hidden(B - 1, c)
            add_y(B - 1)

        @block.scalar
        def _(act):
            def exp_step(u, g, i):
                act.wait_ge(st_done, u * NS + i + 1)
                if i == 0 and not (isinstance(u, int) and u < 2):
                    act.wait_ge(pv_done, u - 1)
                w = 512
                act.activation(pT[:, g % 2, i, 0:w], st_b[i % 2][:, 0:w], ACT.Exp, scale=SCALE).then_inc(exp_done, 1)

            def copy_out(dst, src, wait, n, done):
                act.wait_ge(wait, n)
                act.activation(dst, src, ACT.Copy).then_inc(done, 1)

            def max_rows(u, b, g):
                if not (isinstance(u, int) and u == 0):
                    act.wait_ge(m_in[(g - 1) % 2], 16 * (G // 2 * b + (g + 1) // 2))
                copy_out(mT[:, :], m_b[0][0:3 * UH * NB, 0:P // 2].bitcast(BF16), mt_done, u + 1, mtc_done)

            def xn_T(b):
                if not (isinstance(b, int) and b == 0):
                    act.wait_ge(proj_done, 5 * b)
                copy_out(xnT[:, :], m_b[1][:, :], xt_done, b + 1, xtc_done)

            def v_copy(b):
                if not (isinstance(b, int) and b == 0):
                    act.wait_ge(va_done, b)
                copy_out(v_nat[:, :, :].rearrange("p i d -> p (i d)"), m_b[0][:, :], proj_done, 5 * b + 5, vc_done)

            def o_copy(b, t):
                copy_out(o_sb[:, t, :], o_b[t][:, :], pv_done, G * b + 2 * t + 2, oc_done)

            def on_T(b):
                copy_out(oT[:, :], m_b[0][:, :], ont_done, b + 1, ontc_done)

            def xn2_T(b):
                copy_out(xn2T[:, :], m_b[1][:, :], x2t_done, b + 1, x2tc_done)

            def tanh(b, c):
                act.wait_ge(gu_done, 2 * (NC * b + c) + 1)
                act.activation(th[:, :], m_b[0][:, :], ACT.Tanh, scale=0.5).then_inc(tanh_done, 1)

            def body(b, first, last):
                for g in range(G):
                    u = b * G + g
                    for p in range(POS):
                        if p == 0 and g == 3:
                            o_copy(b, 0)
                        if p == 1:
                            max_rows(u, b, g)
                        if g == 0 and not last and p == 3:
                            xn_T(b + 1)
                        if g == 0 and not first and p == 9:
                            o_copy(b - 1, 1)
                        if g == 1 and not first and p == 6:
                            on_T(b - 1)
                        if g == 1 and not last and p == 11:
                            v_copy(b + 1)
                        if g == 2 and not first:
                            if p == 4:
                                xn2_T(b - 1)
                            if p in (6, 10):
                                tanh(b - 1, (6, 10).index(p))
                        if g == 3 and not first and p == 4:
                            tanh(b - 1, 2)
                        if p >= ST_AT:
                            exp_step(u, g, p - ST_AT)

            xn_T(0)
            v_copy(0)
            body(0, True, False)
            with act.Fori(1, B - 1) as b:
                body(b, False, False)
            body(B - 1, False, True)
            o_copy(B - 1, 1)
            on_T(B - 1)
            xn2_T(B - 1)
            for c in range(NC):
                tanh(B - 1, c)

        @block.gpsimd
        def _(pool):
            def wait(signal, n):
                if not isinstance(n, int):
                    n = pool.to_reg(n)
                    pool.wait_ge(clear_done, 1)
                pool.wait_ge(signal, n)

            def split_max(u):
                wait(max_done, NN * (u + 1))
                if not (isinstance(u, int) and u == 0):
                    wait(mt_done, u)
                pool.tensor_copy(m_parts[:, 0, :], m_row[:, :]).then_inc(mp, 1)
                wait(mp, MP * u + 1)
                pool.tensor_tensor(m_rest[:, :], m_row[:, :], m_parts[:, 0, :], ALU.subtract).then_inc(mp, 1)
                wait(mp, MP * u + 2)
                pool.tensor_copy(m_parts[:, 1, :], m_rest[:, :]).then_inc(mp, 1)
                wait(mp, MP * u + 3)
                pool.tensor_tensor(m_parts[:, 2, :], m_rest[:, :], m_parts[:, 1, :], ALU.subtract).then_inc(mp, 1)

            def causal(u, g, n):
                lo, hi, cols, need = [(0, 4, [0], 4), (4, 8, [0, 384], 8), (8, 10, [0, 256], 10)][n]
                wait(exp_done, NS * u + need)
                for c in cols:
                    v = pT[:, g % 2, lo:hi, c:c + P]
                    pool.affine_select(out=v, in_=v, compare_op=ALU.is_ge, fill=0.0, base=0,
                                       pattern=[[0, hi - lo], [1, P]], channel_multiplier=-1).then_inc(mask_done, 1)

            def lay_values(b, first):
                wait(vc_done, b + 1)
                if not first:
                    wait(pv_done, G * b)
                va = v_aug[:, :, :, :].rearrange("p k (t s a) e -> p (k t) s a e", t=2, s=2)
                vn = v_nat[:, :, :].rearrange("p k (t s a e) -> p (k t) s a e", t=2, s=2, a=UH)
                for s in range(2):
                    last = pool.tensor_copy(va[:, :, s, :, 16 * s:16 * s + DH], vn[:, :, s, :, :])
                last.then_inc(va_done, 1)

            def split_rot(b, w):
                n = SPLIT * (2 * b + w)
                q = rest[:, w, :]
                wait(rot_done, 4 * b + 2 * w + 2)
                if not (isinstance(b, int) and b == 0):
                    wait((scr_q, scr_k)[w], 16 * TERMS * b)
                pool.tensor_tensor(q, rot[:, 2 * w, :], rot[:, 2 * w + 1, :], ALU.add).then_inc(split, 1)
                wait(split, n + 1)
                pool.tensor_copy(parts[:, w, 0, :], q).then_inc(split, 1)
                wait(split, n + 2)
                pool.tensor_tensor(q, q, parts[:, w, 0, :], ALU.subtract).then_inc(split, 1)
                wait(split, n + 3)
                pool.tensor_copy(parts[:, w, 1, :], q).then_inc(split, 1)
                wait(split, n + 4)
                pool.tensor_tensor(parts[:, w, 2, :], q, parts[:, w, 1, :], ALU.subtract).then_inc(split, 1)

            def root(b, mv, rs, step, done):
                wait(step, 2 * b + 2)
                pool.tensor_scalar(rs[:, :], mv[:, :, 1], EPS, None, ALU.add).then_inc(done, 1)
                wait(done, 2 * b + 1)
                pool.tensor_tensor(rs[:, :], rs[:, :], power[:, :], ALU.pow).then_inc(done, 1)

            def root1(b):
                if not (isinstance(b, int) and b == 0):
                    wait(xn_done, b)
                root(b, mean_var, rstd, ln1, rs1_done)

            def root2(b):
                root(b, mean_var2, rstd2, ln2, rs2_done)

            def body(b, first, last):
                for g in range(G):
                    u = b * G + g
                    if g == 0 and not last:
                        root1(b + 1)
                    if g == 2 and not first:
                        root2(b - 1)
                    causal(u, g, 0)
                    if not (last and g == G - 1):
                        split_max(u + 1)
                    if g == 1 and not last:
                        split_rot(b + 1, 1)
                    causal(u, g, 1)
                    causal(u, g, 2)
                    if g == 0:
                        lay_values(b, first)
                        if not last:
                            split_rot(b + 1, 0)

            pool.memset(minus[:, :], -1.0).then_inc(clear_done, 1)
            pool.memset(power[:, :], -0.5).then_inc(clear_done, 1)
            pool.memset(kx[:, :, :].rearrange("p h t -> p (h t)").bitcast(F32), 0.0).then_inc(clear_done, 1)
            pool.memset(qx[:, :, :].rearrange("p h t -> p (h t)").bitcast(F32), 0.0).then_inc(clear_done, 1)
            wait(clear_done, 4)
            root1(0)
            split_rot(0, 0)
            split_rot(0, 1)
            pool.memset(v_aug[:, :, :, :], 0.0).then_inc(clear_done, 1)
            wait(clear_done, 5)
            va = v_aug[:, :, :, :].rearrange("p k (t s a) e -> p (k t) s a e", t=2, s=2)
            for s in range(2):
                last = pool.memset(va[:, :, s, :, 16 * s + DH:16 * s + DH + 1], 1.0)
            last.then_inc(clear_done, 1)
            split_max(0)
            body(0, True, False)
            with pool.Fori(1, B - 1) as b:
                body(b, False, False)
            body(B - 1, False, True)
            root2(B - 1)

        @block.sync
        def _(sp):
            def scratch(b, w):
                sp.wait_ge(split, SPLIT * (2 * b + w + 1))
                scr, part, done = ((q_scr, Q_PART, scr_q), (k_scr, K_PART, scr_k))[w]
                for t in range(TERMS):
                    sp.dma_start(scr[b, DH * t:DH * t + DH].rearrange("i h c -> h i c"),
                                 parts[:, w, part[t], :]).then_inc(done, 16)

            def load_pair(b, t):
                if not (isinstance(b, int) and b == 0):
                    sp.wait_ge(st_done, NS * (G * (b - 1) + 2 * t + 2))
                sp.wait_ge(scr_q, 16 * TERMS * (b + 1))
                sp.wait_ge(scr_k, 16 * TERMS * (b + 1))
                sp.dma_start(qx[0:XR + MR, 8 * t:8 * t + 8, :], q_scr[b, :, 8 * t:8 * t + 8, :]).then_inc(pair_in[t], 16)
                sp.dma_start(kx[0:XR, 8 * t:8 * t + 8, :], k_scr[b, :, 8 * t:8 * t + 8, :]).then_inc(pair_in[t], 16)

            def max_rows(u, g):
                sp.wait_ge(mtc_done, u + 1)
                sp.dma_start(qx[XR:XR + MR, UH * g:UH * g + UH, :], mT[:, :]).then_inc(m_in[g % 2], 16)

            def store(b):
                sp.wait_ge(y_done, b + 1)
                sp.dma_start(out_v[b], x2[:, :, :]).then_inc(stored, 16)
                n = 16 * (b + 1) if isinstance(b, int) else sp.to_reg(16 * (b + 1))
                sp.wait_ge(zero_w, 16 * B)
                sp.wait_ge(stored, n)

            def body(b, first, last):
                for g in range(G):
                    max_rows(b * G + g, g)
                    if g == 0 and not first:
                        load_pair(b, 1)
                    if g == 1 and not last:
                        scratch(b + 1, 0)
                    if g == 2 and not last:
                        scratch(b + 1, 1)
                        load_pair(b + 1, 0)
                    if g == 3 and not first:
                        store(b - 1)

            sp.dma_start(x_sb[:, 0:NB, :], x_v[0]).then_inc(x0_in, 16)
            for dst, src in ((ident, ident_d), (mask, mask_d), (cos, cos_d), (sin, sin_d)):
                sp.dma_start(dst[:, :], src).then_inc(c_in, 16)
            for n, src in enumerate((WqT, WqsT, WkT, WksT, WvT, WoT)):
                sp.dma_start(w_proj[:, n, :], src).then_inc(w_in, 16)
            sp.dma_start(w_int[:, 0, :], WgT).then_inc(wi_in, 16)
            sp.dma_start(w_int[:, 1, :], WuT).then_inc(wi_in, 16)
            sp.dma_start(w_int[:, 2, :].rearrange("p (c d) -> p c d", c=NC),
                         WdT.rearrange("(c p) d -> p c d", p=P)).then_inc(wi_in, 16)
            for b in range(1, B):
                sp.dma_start(x_sb[:, NB * b:NB * b + NB, :], x_v[b]).then_inc(x_in, 16)
            sp.wait_ge(clear_done, 4)
            sp.dma_start(kx[XR:XR + MR, 0:8, :], minus[0:24, :]).then_inc(ones_in, 16)
            sp.dma_start(kx[XR:XR + MR, 8:16, :], minus[0:24, :]).then_inc(ones_in, 16)
            for b in range(B):
                sp.dma_start(q_scr[b, XR:XR + MR], qx[64:64 + MR, :, :]).then_inc(zero_w, 16)
            sp.wait_ge(zero_w, 16 * B)
            scratch(0, 0)
            scratch(0, 1)
            load_pair(0, 0)
            load_pair(0, 1)
            body(0, True, False)
            with sp.Fori(1, B - 1) as b:
                body(b, False, False)
            body(B - 1, False, True)
            store(B - 1)




def kernel(**inputs):
    import numpy as np
    import concourse.bacc as bacc
    from concourse import mybir as mb
    from concourse.bass_utils import run_bass_kernel_spmd as run

    def turned(name, order=None):
        w = np.asarray(inputs[name])
        return np.ascontiguousarray((w if order is None else w[order]).T)

    swap = np.arange(D) ^ 1
    arrays = {
        "x": np.ascontiguousarray(inputs["L0_attn_X"]),
        "wq": turned("L0_attn_W_q"), "wqs": turned("L0_attn_W_q", swap),
        "wk": turned("L0_attn_W_k"), "wks": turned("L0_attn_W_k", swap),
        "wv": turned("L0_attn_W_v"), "wo": turned("L0_attn_W_o"),
        "wg": turned("L0_ffn_w_gate"), "wu": turned("L0_ffn_w_up"), "wd": turned("L0_ffn_w_down"),
    }
    theta = np.float32(10000.0) ** (np.float32(-2.0) * np.arange(DH // 2, dtype=np.float32) / np.float32(DH))
    angle = np.arange(T, dtype=np.float32)[None, :] * theta.astype(np.float32)[:, None]
    row = (np.arange(D) % DH) // 2
    sign = np.where(np.arange(D) % 2 == 0, -1.0, 1.0).astype(np.float32)[:, None]
    arrays["cos"] = np.cos(angle)[row].astype(np.float32)
    arrays["sin"] = (np.sin(angle)[row] * sign).astype(np.float32)
    arrays["ident"] = np.eye(P, dtype=np.float32)
    arrays["mask"] = np.triu(np.full((P, P), MASKED, np.float32), 1)

    nc = bacc.Bacc("TRN2", target_bir_lowering=False, num_devices=1)
    args = [nc.dram_tensor(f"in_{n}", a.shape, mb.dt.from_np(a.dtype), kind="ExternalInput").ap()
            for n, a in arrays.items()]
    args.append(nc.dram_tensor("out_0", (B, T, D), mb.dt.float32, kind="ExternalOutput").ap())
    layer_kernel(nc, *args)
    r = run(nc, [{f"in_{n}": a for n, a in arrays.items()}], core_ids=[0])
    return r.results[0]["out_0"]
```

```python
from contextlib import ExitStack

import concourse.bass as bass
from concourse import mybir

B, T, D = 4, 512, 128
H, DH = 16, 8
P = 128
NB = T // P
HID = 384
NC = HID // P
UH = 4
G = H // UH
EPS = 1e-5
SCALE = float(DH) ** -0.5
W_SCALE = 1.0 / 127.0
MASKED = -1e30

RUNS = [(3, 0), (2, 1), (1, 2)]
TERMS = sum(n for n, _ in RUNS)
XR = TERMS * DH
MR = 3

NAT = [(3, a, 1) for a in range(4)] + [(2, a, 1) for a in range(4)] + [(1, 0, 2), (1, 2, 2), (0, 0, 4)]
STS = ([[(a, 0, 0)] for a in range(4)] + [[(a, 1, 0), (a, 3, 384)] for a in range(4)]
       + [[(2 * p, 2, 0), (2 * p + 1, 2, 256)] for p in range(2)])
PLACE = {(a, kb): (n, c) for n, pieces in enumerate(STS) for a, kb, c in pieces}
NN, NS = len(NAT), len(STS)
POS = 14
ST_AT = 4
PV_AT = {3: 0, 5: 1, 7: 3, 9: 2}


def layer_kernel(nc, X_d, WqT, WqsT, WkT, WksT, WvT, WoT, WgT, WuT, WdT, cos_d, sin_d, ident_d, mask_d, out_d):
    F32, BF16, I32 = mybir.dt.float32, mybir.dt.bfloat16, mybir.dt.int32
    ALU, ACT, AX = mybir.AluOpType, mybir.ActivationFunctionType, mybir.AxisListType

    x_v = X_d.rearrange("b (i p) d -> b p i d", p=P)
    out_v = out_d.rearrange("b (i p) d -> b p i d", p=P)
    q_scr = nc.dram_tensor("q_scr", [B, D, TERMS, T], BF16, kind="Internal").ap()
    k_scr = nc.dram_tensor("k_scr", [B, D, TERMS, T], BF16, kind="Internal").ap()

    ctx = ExitStack()
    with ctx:
        def sb(name, shape, dt=F32):
            return ctx.enter_context(nc.sbuf_tensor(name, shape, dt))

        def sem(name):
            return ctx.enter_context(nc.semaphore(name))

        def bank(name):
            return ctx.enter_context(nc.psum_tensor(name, [P, T], F32))

        x_sb = sb("x_sb", [P, B * NB, D])
        w_proj = sb("w_proj", [P, 6, D])
        w_int = sb("w_int", [P, 3, HID], I32)
        w_ffn = sb("w_ffn", [P, 3, HID])
        cos, sin = sb("cos", [P, T]), sb("sin", [P, T])
        ident, ident16 = sb("ident", [P, P]), sb("ident16", [P, P], BF16)
        mask, mask16 = sb("mask", [P, P]), sb("mask16", [P, P], BF16)
        minus, zeros = sb("minus", [P, T], BF16), sb("zeros", [P, T], BF16)
        qx, kx = sb("qx", [P, H, T], BF16), sb("kx", [P, H, T], BF16)
        stats, mean_var, rstd = sb("stats", [P, NB, 6]), sb("mean_var", [P, NB, 2]), sb("rstd", [P, NB])
        stats2, mean_var2, rstd2 = sb("stats2", [P, NB, 6]), sb("mean_var2", [P, NB, 2]), sb("rstd2", [P, NB])
        power = sb("power", [P, NB])
        xn, xnT = sb("xn", [P, NB, D]), sb("xnT", [P, T])
        rot = sb("rot", [P, 4, T])
        rest = sb("rest", [P, 2, T])
        parts = sb("parts", [P, 2, 3, T], BF16)
        v_nat = sb("v_nat", [P, NB, D])
        v_aug = sb("v_aug", [P, NB, H, 32])
        m_row = sb("m_row", [P, UH * NB])
        m_rest = sb("m_rest", [P, UH * NB])
        m_parts = sb("m_parts", [P, 3, UH * NB], BF16)
        mT = sb("mT", [3 * UH * NB, P], BF16)
        pT = sb("pT", [P, 2, NS, T])
        o_sb = sb("o_sb", [P, 2, T])
        denom = sb("denom", [P, NB, 8])
        o_nat, oT = sb("o_nat", [P, NB, D]), sb("oT", [P, T])
        x2, xn2, xn2T = sb("x2", [P, NB, D]), sb("xn2", [P, NB, D]), sb("xn2T", [P, T])
        th, gated = sb("th", [P, T]), sb("gated", [P, T])
        hT = sb("hT", [P, NC, T])

        nat_b = [bank("nat0"), bank("nat1")]
        st_b = [bank("st0"), bank("st1")]
        o_b = [bank("o0"), bank("o1")]
        m_b = [bank("misc0"), bank("misc1")]

        x0_in, x_in, w_in, wi_in = sem("x0_in"), sem("x_in"), sem("w_in"), sem("wi_in")
        c_in, id_in = sem("c_in"), sem("id_in")
        ones_in, scr_q, scr_k = sem("ones_in"), sem("scr_q"), sem("scr_k")
        pair_in = [sem("pair0_in"), sem("pair1_in")]
        m_in = [sem("m_in0"), sem("m_in1")]
        stored = sem("stored")
        nat_done, st_done, pv_done, mt_done = sem("nat_done"), sem("st_done"), sem("pv_done"), sem("mt_done")
        xt_done, proj_done, ot_done, ont_done = sem("xt_done"), sem("proj_done"), sem("ot_done"), sem("ont_done")
        wo_done, x2t_done, gu_done, down_done = sem("wo_done"), sem("x2t_done"), sem("gu_done"), sem("down_done")
        max_done, rot_done, const_done = sem("max_done"), sem("rot_done"), sem("const_done")
        ln1, ln2, xn_done, xn2_done = sem("ln1"), sem("ln2"), sem("xn_done"), sem("xn2_done")
        denom_done, onat_done, x2_done = sem("denom_done"), sem("onat_done"), sem("x2_done")
        gated_done, h_done, y_done = sem("gated_done"), sem("h_done"), sem("y_done")
        exp_done, mtc_done, xtc_done, vc_done = sem("exp_done"), sem("mtc_done"), sem("xtc_done"), sem("vc_done")
        oc_done, ontc_done, x2tc_done, tanh_done = sem("oc_done"), sem("ontc_done"), sem("x2tc_done"), sem("tanh_done")
        clear_done, mp, mask_done = sem("clear_done"), sem("mp"), sem("mask_done")
        split = [sem("split_q"), sem("split_k")]
        va_done, rs1_done, rs2_done = sem("va_done"), sem("rs1_done"), sem("rs2_done")
        MASKS = 5
        CLEARED = 7
        MP, SPLIT = 4, 5

        block = ctx.enter_context(nc.Block())

        @block.tensor
        def _(pe):
            def nat_step(u, g, i):
                j, a0, n = NAT[i]
                w = P * (j + 1)
                out = nat_b[(i + g * NN) % 2]
                pe.wait_ge(max_done, u * NN + i - 1) if not (isinstance(u, int) and u * NN + i < 2) else None
                o3 = out[:, 0:n * w].rearrange("p (a k) -> p a k", a=n)
                pe.matmul(o3[:, :, P * j:w], ident16[:, :],
                          mask16[:, :].unsqueeze(1).broadcast_to([P, n, P]) if n > 1 else mask16[:, :].unsqueeze(1),
                          start=True, stop=False, skip_group_check=True)
                for a in range(n):
                    h = UH * g + a0 + a
                    mm = pe.matmul(o3[:, a, :], qx[:, h, P * j:P * j + P], kx[:, h, 0:w],
                                   start=False, stop=True, skip_group_check=True)
                mm.then_inc(nat_done, 1)

            def st_step(u, b, g, i):
                if i == 0:
                    pe.wait_ge(m_in[g % 2], 16 * (G // 2 * b + g // 2 + 1))
                if not (isinstance(u, int) and u * NS + i < 2):
                    pe.wait_ge(exp_done, u * NS + i - 1)
                for a, kb, c in STS[i]:
                    h = UH * g + a
                    mm = pe.matmul(st_b[i % 2][:, c:c + T - P * kb], kx[:, h, P * kb:P * kb + P],
                                   qx[:, h, P * kb:T], start=True, stop=True)
                mm.then_inc(st_done, 1)

            def pv_step(u, g, kb, b, first):
                need = {0: 1, 1: 3, 3: 3, 2: 5}[kb]
                pe.wait_ge(mask_done, u * MASKS + need)
                if kb == 0 and g == 0:
                    pe.wait_ge(va_done, b + 1)
                if kb == 0 and g % 2 == 0 and not first:
                    pe.wait_ge(oc_done, 2 * b + g // 2 - 1)
                for a in range(UH):
                    n, c = PLACE[a, kb]
                    mm = pe.matmul(o_b[g // 2][32 * a:32 * a + 32, P * kb:T], v_aug[:, kb, UH * g + a, :],
                                   pT[:, g % 2, n, c:c + T - P * kb],
                                   start=(g % 2 == 0 and kb == 0), stop=(g % 2 == 1 and kb == 2),
                                   skip_group_check=True)
                if kb == 2:
                    mm.then_inc(pv_done, 1)

            def max_T(u):
                n = MP * (u + 1) if isinstance(u, int) else pe.to_reg(MP * (u + 1))
                pe.wait_ge(const_done, 1)
                pe.wait_ge(mp, n)
                pe.transpose(m_b[0][0:3 * UH * NB, 0:P // 2].bitcast(BF16),
                             m_parts[:, :, :].rearrange("p c m -> p (c m)"), ident16[:, :]).then_inc(mt_done, 1)

            def four_T(out, src, done):
                for i in range(NB):
                    mm = pe.transpose(out[:, P * i:P * i + P], src(i), ident[:, :])
                mm.then_inc(done, 1)

            def xn_T(b):
                pe.wait_ge(xn_done, b + 1)
                four_T(m_b[1], lambda i: xn[:, i, :], xt_done)

            def project(b, n):
                if n == 0:
                    pe.wait_ge(xtc_done, b + 1)
                if n < 4:
                    pe.matmul(m_b[n % 2][:, :], w_proj[:, n, :], xnT[:, :], start=True, stop=True).then_inc(proj_done, 1)
                else:
                    for i in range(NB):
                        mm = pe.matmul(m_b[0][:, P * i:P * i + P], xnT[:, P * i:P * i + P], w_proj[:, 4, :],
                                       start=True, stop=True)
                    mm.then_inc(proj_done, 1)

            def o_T(b, t):
                pe.wait_ge(oc_done, 2 * b + t + 1)
                four_T(m_b[1], lambda i: o_sb[:, t, P * i:P * i + P], ot_done)

            def on_T(b):
                pe.wait_ge(onat_done, 2 * b + 2)
                four_T(m_b[0], lambda i: o_nat[:, i, :], ont_done)

            def w_o(b):
                pe.wait_ge(ontc_done, b + 1)
                for i in range(NB):
                    mm = pe.matmul(m_b[1][:, P * i:P * i + P], oT[:, P * i:P * i + P], w_proj[:, 5, :],
                                   start=True, stop=True)
                mm.then_inc(wo_done, 1)

            def xn2_T(b):
                pe.wait_ge(xn2_done, b + 1)
                four_T(m_b[1], lambda i: xn2[:, i, :], x2t_done)

            def gate_up(b, c):
                if c == 0:
                    pe.wait_ge(x2tc_done, b + 1)
                else:
                    pe.wait_ge(h_done, NC * b + c)
                for n in range(2):
                    pe.matmul(m_b[n][:, :], w_ffn[:, n, P * c:P * c + P], xn2T[:, :],
                              start=True, stop=True).then_inc(gu_done, 1)

            def down(b):
                pe.wait_ge(h_done, NC * b + NC)
                for i in range(NB):
                    for c in range(NC):
                        mm = pe.matmul(m_b[0][:, P * i:P * i + P], hT[:, c, P * i:P * i + P],
                                       w_ffn[:, 2, P * c:P * c + P], start=(c == 0), stop=(c == NC - 1))
                mm.then_inc(down_done, 1)

            def body(b, first, last):
                for g in range(G):
                    u = b * G + g
                    for p in range(POS):
                        if p < NN and not (last and g == G - 1):
                            ng = (g + 1) % G
                            nb_ = b + 1 if g == G - 1 else b
                            if p == 0 and ng % 2 == 0:
                                pe.wait_ge(pair_in[ng // 2], 48 * nb_ + 32)
                            nat_step(u + 1, ng, p)
                        if p in PV_AT and not (first and g == 0):
                            pv_step(u - 1, (g - 1) % G, PV_AT[p], b - 1 if g == 0 else b,
                                    first if g else False)
                        if p == 1:
                            if g == 0 and not first:
                                pe.wait_ge(mtc_done, u)
                            if g == 1 and not last:
                                pe.wait_ge(rot_done, 4 * (b + 1) + 3)
                            if g == 1 and last:
                                pe.wait_ge(mtc_done, u)
                            if g == 2 and not last:
                                pe.wait_ge(vc_done, b + 2)
                            if g == 2 and last:
                                pe.wait_ge(ontc_done, b)
                            if g == 3 and not first:
                                pe.wait_ge(h_done, NC * (b - 1) + 2)
                            if g == 3 and first:
                                pe.wait_ge(mtc_done, u)
                            max_T(u)
                        if g == 0 and not last:
                            if p == 3:
                                xn_T(b + 1)
                            if p == 5:
                                pe.wait_ge(mtc_done, u + 1)
                                project(b + 1, 0)
                            if p == 6:
                                project(b + 1, 1)
                            if p == 8:
                                pe.wait_ge(rot_done, 4 * (b + 1) + 1)
                                project(b + 1, 2)
                            if p == 9:
                                pe.wait_ge(rot_done, 4 * (b + 1) + 2)
                                project(b + 1, 3)
                        if g == 0 and not first and p == 12:
                            if last:
                                pe.wait_ge(h_done, NC * (b - 1))
                            else:
                                pe.wait_ge(rot_done, 4 * (b + 1) + 4)
                            o_T(b - 1, 0)
                        if g == 1 and not first:
                            if p == 3:
                                pe.wait_ge(onat_done, 2 * (b - 1) + 1)
                                o_T(b - 1, 1)
                            if p == 6:
                                pe.wait_ge(mtc_done, u + 1)
                                on_T(b - 1)
                            if p == 9:
                                w_o(b - 1)
                        if g == 1 and not last and p == 11:
                            if first:
                                pe.wait_ge(mtc_done, u + 1)
                            else:
                                pe.wait_ge(ontc_done, b)
                            project(b + 1, 4)
                        if g == 2 and not first:
                            if p == 3:
                                xn2_T(b - 1)
                            if p == 6:
                                pe.wait_ge(mtc_done, u + 1)
                                gate_up(b - 1, 0)
                            if p == 10:
                                gate_up(b - 1, 1)
                        if g == 3 and not first:
                            if p == 4:
                                pe.wait_ge(mtc_done, u + 1)
                                gate_up(b - 1, 2)
                            if p == 9:
                                down(b - 1)
                        if p >= ST_AT:
                            st_step(u, b, g, p - ST_AT)

            pe.wait_ge(id_in, 16)
            xn_T(0)
            pe.wait_ge(w_in, 16 * 6)
            project(0, 0)
            project(0, 1)
            pe.wait_ge(rot_done, 1)
            project(0, 2)
            pe.wait_ge(rot_done, 2)
            project(0, 3)
            pe.wait_ge(rot_done, 3)
            project(0, 4)
            pe.wait_ge(const_done, 2)
            pe.wait_ge(ones_in, 32)
            pe.wait_ge(pair_in[0], 32)
            for i in range(NN):
                nat_step(0, 0, i)
            pe.wait_ge(vc_done, 1)
            pe.wait_ge(rot_done, 4)
            pe.wait_ge(const_done, 3)
            body(0, True, False)
            with pe.Fori(1, B - 1) as b:
                body(b, False, False)
            body(B - 1, False, True)
            for kb in (0, 1, 3, 2):
                pv_step(B * G - 1, G - 1, kb, B - 1, False)
            pe.wait_ge(h_done, NC * (B - 1))
            o_T(B - 1, 0)
            pe.wait_ge(onat_done, 2 * B - 1)
            o_T(B - 1, 1)
            pe.wait_ge(y_done, B - 1)
            on_T(B - 1)
            w_o(B - 1)
            xn2_T(B - 1)
            for c in range(NC):
                gate_up(B - 1, c)
            down(B - 1)

        @block.vector
        def _(dve):
            def row_max(u, g, i):
                j, a0, n = NAT[i]
                w = P * (j + 1)
                dve.wait_ge(nat_done, u * NN + i + 1)
                if i == 0 and not (isinstance(u, int) and u == 0):
                    dve.wait_ge(mp, MP * u)
                dve.reduce_max(m_row[:, NB * a0 + j:NB * (a0 + n - 1) + j + 1:NB],
                               nat_b[(i + g * NN) % 2][:, 0:n * w].rearrange("p (a k) -> p a k", a=n),
                               AX.X).then_inc(max_done, 1)

            def moments(b, src, st, mv, step):
                for i in range(NB):
                    last = dve.bn_stats(st[:, i, :], src(i))
                last.then_inc(step, 1)
                n = 2 * b + 1 if isinstance(b, int) else dve.to_reg(2 * b + 1)
                dve.wait_ge(x0_in, 16)
                dve.wait_ge(step, n)
                for i in range(NB):
                    last = dve.bn_aggr(mv[:, i, :], st[:, i, :])
                last.then_inc(step, 1)

            def centre(b, src, mv, rs, dst, rstd_done, done):
                dve.wait_ge(rstd_done, 2 * b + 2)
                for i in range(NB):
                    last = dve.tensor_scalar(dst[:, i, :], src(i), mv[:, i, 0:1], rs[:, i:i + 1],
                                             ALU.subtract, ALU.mult)
                last.then_inc(done, 1)

            xs = x_sb[:, :, :].rearrange("p (b i) d -> p b i d", b=B)

            def moments1(b):
                moments(b, lambda i: xs[:, b, i, :], stats, mean_var, ln1)

            def centre1(b):
                if not (isinstance(b, int) and b == 0):
                    dve.wait_ge(xt_done, b)
                centre(b, lambda i: xs[:, b, i, :], mean_var, rstd, xn, rs1_done, xn_done)

            def moments2(b):
                moments(b, lambda i: x2[:, i, :], stats2, mean_var2, ln2)

            def centre2(b):
                centre(b, lambda i: x2[:, i, :], mean_var2, rstd2, xn2, rs2_done, xn2_done)

            def rotate(b, n):
                dve.wait_ge(proj_done, 5 * b + n + 1)
                if n % 2 == 0 and not (isinstance(b, int) and b == 0):
                    dve.wait_ge(split[n // 2], SPLIT * (b - 1) + 1)
                dve.tensor_tensor(rot[:, n, :], m_b[n % 2][:, :], (cos if n % 2 == 0 else sin)[:, :],
                                  ALU.mult).then_inc(rot_done, 1)

            def normalise(b, t):
                dve.wait_ge(ot_done, 2 * b + t + 1)
                o4 = m_b[1][:, :].rearrange("p (i a s e) -> p i a s e", i=NB, a=UH, s=2)
                dn = denom[:, :, :].rearrange("p i (a s) -> p i a s", s=2)
                dve.reciprocal(dn, o4[:, :, :, :, DH]).then_inc(denom_done, 1)
                dve.wait_ge(denom_done, 2 * b + t + 1)
                on = o_nat[:, :, :].rearrange("p i (t s a e) -> p i t s a e", t=2, s=2, a=UH)
                for s in range(2):
                    last = dve.tensor_tensor(on[:, :, t, s, :, :], o4[:, :, :, s, 0:DH],
                                             dn[:, :, :, s].unsqueeze(3).broadcast_to([P, NB, UH, DH]), ALU.mult)
                last.then_inc(onat_done, 1)

            def add_x(b):
                dve.wait_ge(wo_done, b + 1)
                xs = x_sb[:, :, :].rearrange("p (b n) d -> p b (n d)", b=B)
                dve.tensor_tensor(x2[:, :, :].rearrange("p i d -> p (i d)"), m_b[1][:, :], xs[:, b, :],
                                  ALU.add).then_inc(x2_done, 1)
                dve.wait_ge(x2_done, b + 1)

            def hidden(b, c):
                dve.wait_ge(tanh_done, NC * b + c + 1)
                dve.scalar_tensor_tensor(gated[:, :], th[:, :], 1.0, m_b[0][:, :], ALU.add,
                                         ALU.mult).then_inc(gated_done, 1)
                dve.wait_ge(gated_done, NC * b + c + 1)
                dve.wait_ge(gu_done, 2 * (NC * b + c) + 2)
                dve.scalar_tensor_tensor(hT[:, c, :], gated[:, :], 0.5, m_b[1][:, :], ALU.mult,
                                         ALU.mult).then_inc(h_done, 1)

            def add_y(b):
                dve.wait_ge(down_done, b + 1)
                x2f = x2[:, :, :].rearrange("p i d -> p (i d)")
                dve.tensor_tensor(x2f, m_b[0][:, :], x2f, ALU.add).then_inc(y_done, 1)

            def body(b, first, last):
                for g in range(G):
                    u = b * G + g
                    for p in range(POS):
                        if p < NN and not (last and g == G - 1):
                            row_max(u + 1, (g + 1) % G, p)
                        if g == 0 and not last:
                            if p == 0:
                                moments1(b + 1)
                            if p == 2:
                                centre1(b + 1)
                            if p in (5, 6, 8, 9):
                                rotate(b + 1, (5, 6, 8, 9).index(p))
                        if g == 0 and p == 12 and not first:
                            normalise(b - 1, 0)
                        if g == 1 and not first:
                            if p == 3:
                                normalise(b - 1, 1)
                            if p == 9:
                                add_x(b - 1)
                                moments2(b - 1)
                        if g == 2 and not first and p == 1:
                            centre2(b - 1)
                        if g == 2 and not first and p in (6, 10):
                            hidden(b - 1, (6, 10).index(p))
                        if g == 3 and not first:
                            if p == 4:
                                hidden(b - 1, 2)
                            if p == 9:
                                add_y(b - 1)

            dve.wait_ge(x0_in, 16)
            moments1(0)
            centre1(0)
            dve.wait_ge(c_in, 48)
            dve.tensor_copy(ident16[:, :], ident[:, :]).then_inc(const_done, 1)
            dve.tensor_copy(mask16[:, :], mask[:, :]).then_inc(const_done, 1)
            for n in range(4):
                rotate(0, n)
                if n % 2:
                    dve.wait_ge(rot_done, n + 1)
                    dve.tensor_tensor(rest[:, n // 2, :], rot[:, n - 1, :], rot[:, n, :], ALU.add).then_inc(split[n // 2], 1)
            for w in range(2):
                dve.wait_ge(split[w], 2)
                dve.tensor_tensor(rest[:, w, :], rest[:, w, :], parts[:, w, 0, :], ALU.subtract).then_inc(split[w], 1)
                dve.wait_ge(split[w], 4)
                dve.tensor_tensor(parts[:, w, 2, :], rest[:, w, :], parts[:, w, 1, :], ALU.subtract).then_inc(split[w], 1)
            dve.wait_ge(wi_in, 16 * 3)
            dve.tensor_scalar(w_ffn[:, :, :], w_int[:, :, :], W_SCALE, None, ALU.mult).then_inc(const_done, 1)
            dve.wait_ge(x_in, 16 * (B - 1))
            for i in range(NN):
                row_max(0, 0, i)
            body(0, True, False)
            with dve.Fori(1, B - 1) as b:
                body(b, False, False)
            body(B - 1, False, True)
            normalise(B - 1, 0)
            normalise(B - 1, 1)
            dve.wait_ge(stored, 16 * (B - 1))
            add_x(B - 1)
            moments2(B - 1)
            centre2(B - 1)
            for c in range(NC):
                hidden(B - 1, c)
            add_y(B - 1)

        @block.scalar
        def _(act):
            def exp_step(u, g, i):
                act.wait_ge(st_done, u * NS + i + 1)
                if i == 0 and not (isinstance(u, int) and u < 2):
                    act.wait_ge(pv_done, u - 1)
                w = 512
                act.activation(pT[:, g % 2, i, 0:w], st_b[i % 2][:, 0:w], ACT.Exp, scale=SCALE).then_inc(exp_done, 1)

            def copy_out(dst, src, wait, n, done):
                act.wait_ge(wait, n)
                act.activation(dst, src, ACT.Copy).then_inc(done, 1)

            def max_rows(u, b, g):
                if not (isinstance(u, int) and u == 0):
                    act.wait_ge(m_in[(g - 1) % 2], 16 * (G // 2 * b + (g + 1) // 2))
                copy_out(mT[:, :], m_b[0][0:3 * UH * NB, 0:P // 2].bitcast(BF16), mt_done, u + 1, mtc_done)

            def xn_T(b):
                if not (isinstance(b, int) and b == 0):
                    act.wait_ge(proj_done, 5 * b)
                copy_out(xnT[:, :], m_b[1][:, :], xt_done, b + 1, xtc_done)

            def v_copy(b):
                if not (isinstance(b, int) and b == 0):
                    act.wait_ge(va_done, b)
                copy_out(v_nat[:, :, :].rearrange("p i d -> p (i d)"), m_b[0][:, :], proj_done, 5 * b + 5, vc_done)

            def cast(b, w, n):
                done = split[w]
                act.wait_ge(done, SPLIT * b + 2 * n + 1)
                if n == 0 and not (isinstance(b, int) and b == 0):
                    act.wait_ge((scr_q, scr_k)[w], 16 * len(RUNS) * b)
                act.activation(parts[:, w, n, :], rest[:, w, :], ACT.Copy).then_inc(done, 1)

            def lay_values(b, first):
                act.wait_ge(vc_done, b + 1)
                if first:
                    act.wait_ge(clear_done, CLEARED)
                else:
                    act.wait_ge(pv_done, G * b)
                va = v_aug[:, :, :, :].rearrange("p k (t s a) e -> p (k t) s a e", t=2, s=2)
                vn = v_nat[:, :, :].rearrange("p k (t s a e) -> p (k t) s a e", t=2, s=2, a=UH)
                for s in range(2):
                    last = act.activation(va[:, :, s, :, 16 * s:16 * s + DH], vn[:, :, s, :, :], ACT.Copy)
                last.then_inc(va_done, 1)

            def o_copy(b, t):
                copy_out(o_sb[:, t, :], o_b[t][:, :], pv_done, G * b + 2 * t + 2, oc_done)

            def on_T(b):
                copy_out(oT[:, :], m_b[0][:, :], ont_done, b + 1, ontc_done)

            def xn2_T(b):
                copy_out(xn2T[:, :], m_b[1][:, :], x2t_done, b + 1, x2tc_done)

            def tanh(b, c):
                act.wait_ge(gu_done, 2 * (NC * b + c) + 1)
                act.activation(th[:, :], m_b[0][:, :], ACT.Tanh, scale=0.5).then_inc(tanh_done, 1)

            def body(b, first, last):
                for g in range(G):
                    u = b * G + g
                    for p in range(POS):
                        if p == 0 and g == 3:
                            o_copy(b, 0)
                        if p == 1:
                            max_rows(u, b, g)
                        if g == 0 and not last and p == 3:
                            xn_T(b + 1)
                        if g == 0 and not first and p == 9:
                            o_copy(b - 1, 1)
                        if g == 0 and not last and p in (7, 10, 12):
                            cast(b + 1, p // 12, (7, 10, 12).index(p) % 2)
                        if g == 1 and not last and p == 0:
                            cast(b + 1, 1, 1)
                        if g == 0 and p == 11:
                            lay_values(b, first)
                        if g == 1 and not first and p == 6:
                            on_T(b - 1)
                        if g == 1 and not last and p == 11:
                            v_copy(b + 1)
                        if g == 2 and not first:
                            if p == 3:
                                xn2_T(b - 1)
                            if p in (6, 10):
                                tanh(b - 1, (6, 10).index(p))
                        if g == 3 and not first and p == 4:
                            tanh(b - 1, 2)
                        if p >= ST_AT:
                            exp_step(u, g, p - ST_AT)

            xn_T(0)
            for w in range(2):
                for n in range(2):
                    cast(0, w, n)
            v_copy(0)
            body(0, True, False)
            with act.Fori(1, B - 1) as b:
                body(b, False, False)
            body(B - 1, False, True)
            o_copy(B - 1, 1)
            on_T(B - 1)
            xn2_T(B - 1)
            for c in range(NC):
                tanh(B - 1, c)

        @block.gpsimd
        def _(pool):
            def wait(signal, n):
                if not isinstance(n, int):
                    n = pool.to_reg(n)
                    pool.wait_ge(clear_done, 1)
                pool.wait_ge(signal, n)

            def split_max(u):
                wait(max_done, NN * (u + 1))
                if not (isinstance(u, int) and u == 0):
                    wait(mt_done, u)
                pool.tensor_copy(m_parts[:, 0, :], m_row[:, :]).then_inc(mp, 1)
                wait(mp, MP * u + 1)
                pool.tensor_tensor(m_rest[:, :], m_row[:, :], m_parts[:, 0, :], ALU.subtract).then_inc(mp, 1)
                wait(mp, MP * u + 2)
                pool.tensor_copy(m_parts[:, 1, :], m_rest[:, :]).then_inc(mp, 1)
                wait(mp, MP * u + 3)
                pool.tensor_tensor(m_parts[:, 2, :], m_rest[:, :], m_parts[:, 1, :], ALU.subtract).then_inc(mp, 1)

            def causal(u, g, n):
                lo, hi, cols, need = [(0, 4, [0], 4), (4, 8, [0, 384], 8), (8, 10, [0, 256], 10)][n]
                wait(exp_done, NS * u + need)
                for c in cols:
                    v = pT[:, g % 2, lo:hi, c:c + P]
                    pool.affine_select(out=v, in_=v, compare_op=ALU.is_ge, fill=0.0, base=0,
                                       pattern=[[0, hi - lo], [1, P]], channel_multiplier=-1).then_inc(mask_done, 1)

            def split_rot(b, w, stage):
                q, p3, done, n = rest[:, w, :], parts[:, w], split[w], SPLIT * b
                if stage == 0:
                    wait(rot_done, 4 * b + 2 * w + 2)
                    if not (isinstance(b, int) and b == 0):
                        wait(done, n)
                    pool.tensor_tensor(q, rot[:, 2 * w, :], rot[:, 2 * w + 1, :], ALU.add).then_inc(done, 1)
                if stage == 1:
                    wait(done, n + 2)
                    pool.tensor_tensor(q, q, p3[:, 0, :], ALU.subtract).then_inc(done, 1)
                if stage == 2:
                    wait(done, n + 4)
                    pool.tensor_tensor(p3[:, 2, :], q, p3[:, 1, :], ALU.subtract).then_inc(done, 1)

            def root(b, mv, rs, step, done):
                wait(step, 2 * b + 2)
                pool.tensor_scalar(rs[:, :], mv[:, :, 1], EPS, None, ALU.add).then_inc(done, 1)
                wait(done, 2 * b + 1)
                pool.tensor_tensor(rs[:, :], rs[:, :], power[:, :], ALU.pow).then_inc(done, 1)

            def root1(b):
                if not (isinstance(b, int) and b == 0):
                    wait(xn_done, b)
                root(b, mean_var, rstd, ln1, rs1_done)

            def root2(b):
                root(b, mean_var2, rstd2, ln2, rs2_done)

            def body(b, first, last):
                for g in range(G):
                    u = b * G + g
                    if g == 0 and not last:
                        root1(b + 1)
                    prep = g == 0 and not last
                    if prep:
                        split_rot(b + 1, 0, 0)
                    causal(u, g, 0)
                    if prep:
                        split_rot(b + 1, 0, 1)
                    if g == 1 and not last:
                        split_rot(b + 1, 1, 2)
                    if not (last and g == G - 1):
                        split_max(u + 1)
                    if prep:
                        split_rot(b + 1, 0, 2)
                        split_rot(b + 1, 1, 0)
                    if g == 1 and not first:
                        root2(b - 1)
                    causal(u, g, 1)
                    if prep:
                        split_rot(b + 1, 1, 1)
                    causal(u, g, 2)

            def clear(t, value=0.0):
                pool.memset(t, value).then_inc(clear_done, 1)

            clear(power[:, :], -0.5)
            clear(minus[:, :], -1.0)
            clear(zeros[:, :])
            clear(kx[:, :, :].rearrange("p h t -> p (h t)").bitcast(F32))
            root1(0)
            clear(qx[:, :, :].rearrange("p h t -> p (h t)").bitcast(F32))
            clear(v_aug[:, :, :, :])
            pool.wait_ge(clear_done, CLEARED - 1)
            va = v_aug[:, :, :, :].rearrange("p k (t s a) e -> p (k t) s a e", t=2, s=2)
            for s in range(2):
                last = pool.memset(va[:, :, s, :, 16 * s + DH:16 * s + DH + 1], 1.0)
            last.then_inc(clear_done, 1)
            split_max(0)
            body(0, True, False)
            with pool.Fori(1, B - 1) as b:
                body(b, False, False)
            body(B - 1, False, True)
            root2(B - 1)

        @block.sync
        def _(sp):
            def scratch(b, w):
                sp.wait_ge(split[w], SPLIT * (b + 1))
                t = 0
                for n, part in RUNS:
                    src = parts[:, w, part:part + 1, :].broadcast_to([P, n, T]) if w == 0 else parts[:, w, 0:n, :]
                    sp.dma_start((q_scr, k_scr)[w][b, :, t:t + n, :], src).then_inc((scr_q, scr_k)[w], 16)
                    t += n

            def load_pair(b, t):
                if not (isinstance(b, int) and b == 0):
                    sp.wait_ge(st_done, NS * (G * (b - 1) + 2 * t + 2))
                    sp.dma_start(qx[XR:XR + MR, 8 * t:8 * t + 8, :], zeros[0:24, :]).then_inc(pair_in[t], 16)
                for dst, scr, done in ((qx, q_scr, scr_q), (kx, k_scr, scr_k)):
                    sp.wait_ge(done, 16 * len(RUNS) * (b + 1))
                    sp.dma_start(dst[0:XR, 8 * t:8 * t + 8, :],
                                 scr[b, 64 * t:64 * t + 64].rearrange("(h i) t c -> (i t) h c", i=DH)
                                 ).then_inc(pair_in[t], 16)

            def max_rows(u, g):
                sp.wait_ge(mtc_done, u + 1)
                sp.dma_start(qx[XR:XR + MR, UH * g:UH * g + UH, :], mT[:, :]).then_inc(m_in[g % 2], 16)

            def store(b):
                sp.wait_ge(y_done, b + 1)
                sp.dma_start(out_v[b], x2[:, :, :]).then_inc(stored, 16)
                n = 16 * (b + 1) if isinstance(b, int) else sp.to_reg(16 * (b + 1))
                sp.wait_ge(c_in, 48)
                sp.wait_ge(stored, n)

            def body(b, first, last):
                for g in range(G):
                    max_rows(b * G + g, g)
                    if g == 0 and not first:
                        load_pair(b, 1)
                    if g == 1 and not last:
                        scratch(b + 1, 0)
                    if g == 2 and not last:
                        scratch(b + 1, 1)
                        load_pair(b + 1, 0)
                    if g == 3 and not first:
                        store(b - 1)

            sp.dma_start(x_sb[:, 0:NB, :], x_v[0]).then_inc(x0_in, 16)
            sp.dma_start(ident[:, :], ident_d).then_inc(id_in, 16)
            for n, src in enumerate((WqT, WqsT, WkT, WksT, WvT, WoT)):
                sp.dma_start(w_proj[:, n, :], src).then_inc(w_in, 16)
                if n == 1:
                    for dst, csrc in ((cos, cos_d), (sin, sin_d), (mask, mask_d)):
                        sp.dma_start(dst[:, :], csrc).then_inc(c_in, 16)
            sp.dma_start(w_int[:, 0, :], WgT).then_inc(wi_in, 16)
            sp.dma_start(w_int[:, 1, :], WuT).then_inc(wi_in, 16)
            sp.dma_start(w_int[:, 2, :].rearrange("p (c d) -> p c d", c=NC),
                         WdT.rearrange("(c p) d -> p c d", p=P)).then_inc(wi_in, 16)
            for b in range(1, B):
                sp.dma_start(x_sb[:, NB * b:NB * b + NB, :], x_v[b]).then_inc(x_in, 16)
            sp.wait_ge(clear_done, 4)
            sp.dma_start(kx[XR:XR + MR, 0:8, :], minus[0:24, :]).then_inc(ones_in, 16)
            sp.dma_start(kx[XR:XR + MR, 8:16, :], minus[0:24, :]).then_inc(ones_in, 16)
            scratch(0, 0)
            scratch(0, 1)
            sp.wait_ge(clear_done, 5)
            load_pair(0, 0)
            load_pair(0, 1)
            body(0, True, False)
            with sp.Fori(1, B - 1) as b:
                body(b, False, False)
            body(B - 1, False, True)
            store(B - 1)




def kernel(**inputs):
    import numpy as np
    import concourse.bacc as bacc
    from concourse import mybir as mb
    from concourse.bass_utils import run_bass_kernel_spmd as run

    def turned(name, order=None):
        w = np.asarray(inputs[name])
        return np.ascontiguousarray((w if order is None else w[order]).T)

    swap = np.arange(D) ^ 1
    arrays = {
        "x": np.ascontiguousarray(inputs["L0_attn_X"]),
        "wq": turned("L0_attn_W_q"), "wqs": turned("L0_attn_W_q", swap),
        "wk": turned("L0_attn_W_k"), "wks": turned("L0_attn_W_k", swap),
        "wv": turned("L0_attn_W_v"), "wo": turned("L0_attn_W_o"),
        "wg": turned("L0_ffn_w_gate"), "wu": turned("L0_ffn_w_up"), "wd": turned("L0_ffn_w_down"),
    }
    theta = np.float32(10000.0) ** (np.float32(-2.0) * np.arange(DH // 2, dtype=np.float32) / np.float32(DH))
    angle = np.arange(T, dtype=np.float32)[None, :] * theta.astype(np.float32)[:, None]
    row = (np.arange(D) % DH) // 2
    sign = np.where(np.arange(D) % 2 == 0, -1.0, 1.0).astype(np.float32)[:, None]
    arrays["cos"] = np.cos(angle)[row].astype(np.float32)
    arrays["sin"] = (np.sin(angle)[row] * sign).astype(np.float32)
    arrays["ident"] = np.eye(P, dtype=np.float32)
    arrays["mask"] = np.triu(np.full((P, P), MASKED, np.float32), 1)

    nc = bacc.Bacc("TRN2", target_bir_lowering=False, num_devices=1)
    args = [nc.dram_tensor(f"in_{n}", a.shape, mb.dt.from_np(a.dtype), kind="ExternalInput").ap()
            for n, a in arrays.items()]
    args.append(nc.dram_tensor("out_0", (B, T, D), mb.dt.float32, kind="ExternalOutput").ap())
    layer_kernel(nc, *args)
    r = run(nc, [{f"in_{n}": a for n, a in arrays.items()}], core_ids=[0])
    return r.results[0]["out_0"]
```

```python
from contextlib import ExitStack

import concourse.bass as bass
from concourse import mybir

B, T, D = 4, 512, 128
H, DH = 16, 8
P = 128
NB = T // P
HID = 384
NC = HID // P
UH = 4
G = H // UH
EPS = 1e-5
SCALE = float(DH) ** -0.5
W_SCALE = 1.0 / 127.0
MASKED = -1e30

RUNS = [(3, 0), (2, 1), (1, 2)]
TERMS = sum(n for n, _ in RUNS)
XR = TERMS * DH
MR = 3

NAT = [(3, a, 1) for a in range(4)] + [(2, a, 1) for a in range(4)] + [(1, 0, 2), (1, 2, 2), (0, 0, 4)]
STS = ([[(a, 0, 0)] for a in range(4)] + [[(a, 1, 0), (a, 3, 384)] for a in range(4)]
       + [[(2 * p, 2, 0), (2 * p + 1, 2, 256)] for p in range(2)])
NN, NS = len(NAT), len(STS)


def back(seq, k):
    return next(d for d in range(1, len(seq)) if seq[k - d] == seq[k])


NAT_BANKS, ST_BANKS = 2, 3
NAT_SEQ = [k % NAT_BANKS for k in range(G * NN)]
ST_SEQ = [i % ST_BANKS for _ in range(G) for i in range(NS)]
PLACE = {(a, kb): (n, c) for n, pieces in enumerate(STS) for a, kb, c in pieces}
WARM = [14, 8]
POS = 14
HB, HT = NB // 2, T // 2
PROJ_BANK = [1, 0, 1, 0]
ST_AT = 4
PV_AT = {0: 0, 1: 1, 2: 3, 3: 2}
PE_AT = {"max_T": 1,
         "q": 2, "q_swap": 4, "o_T1": 7, "on_T": 9, "w_o": 12,
         "k": 4, "k_swap": 5, "xn2_T": 8, "gate0": 11, "up0": 13,
         "gate1": 4, "up1": 6, "gate2": 8, "up2": 12,
         "down0": 4, "down1": 4, "down2": 6, "down3": 8, "o_T0": 9}
DVE_AT = {"q": 2, "q_swap": 4, "norm1": 7, "add_x": 13, "spread": 13,
          "means": 1, "k": 4, "centre0": 4, "centre1": 6, "k_swap": 5, "gate0": 12, "up0": 13,
          "gate1": 6, "up1": 7, "gate2": 13, "up2": 13,
          "add_y": 8, "norm0": 13}
POOL_ORDER = ["root2", "part0", "causal0", "part1", "max", "causal1", "causal2", "part2"]
ACT_AT = {"max": 3,
          "values": 3, "o_copy1": 4, "q0": 7, "on_T": 9, "q1": 12,
          "xn2_T": 8, "k0": 8, "tanh0": 11, "k1": 13,
          "tanh1": 4, "o_copy0": 8, "tanh2": 10}


def layer_kernel(nc, X_d, w_proj_d, w_ffn_d, ident_d, const_d, out_d):
    F32, BF16, I32 = mybir.dt.float32, mybir.dt.bfloat16, mybir.dt.int32
    ALU, ACT, AX = mybir.AluOpType, mybir.ActivationFunctionType, mybir.AxisListType

    x_v = X_d.rearrange("b (i p) d -> b p i d", p=P)
    out_v = out_d.rearrange("b (i p) d -> b p i d", p=P)
    q_scr = nc.dram_tensor("q_scr", [B, D, TERMS, T], BF16, kind="Internal").ap()
    k_scr = nc.dram_tensor("k_scr", [B, D, TERMS, T], BF16, kind="Internal").ap()

    ctx = ExitStack()
    with ctx:
        def sb(name, shape, dt=F32):
            return ctx.enter_context(nc.sbuf_tensor(name, shape, dt))

        def sem(name):
            return ctx.enter_context(nc.semaphore(name))

        def bank(name):
            return ctx.enter_context(nc.psum_tensor(name, [P, T], F32))

        x_sb = sb("x_sb", [P, B * NB, D])
        w_proj = sb("w_proj", [P, 6, D])
        w_int = sb("w_int", [P, 3, HID], I32)
        w_ffn = sb("w_ffn", [P, 3, HID])
        const = sb("const", [P, 2 * T + P])
        cos, sin, mask = const[:, 0:T], const[:, T:2 * T], const[:, 2 * T:2 * T + P]
        ident, ident16 = sb("ident", [P, P]), sb("ident16", [P, P], BF16)
        mask16 = sb("mask16", [P, P], BF16)
        minus, zeros = sb("minus", [P, T], BF16), sb("zeros", [P, T], BF16)
        qx, kx = sb("qx", [P, H, T], BF16), sb("kx", [P, H, T], BF16)
        stats, mean_var = sb("stats", [P, B * NB, 6]), sb("mean_var", [P, B * NB, 2])
        rstd = sb("rstd", [P, B * NB])
        stats2, mean_var2, rstd2 = sb("stats2", [P, NB, 6]), sb("mean_var2", [P, NB, 2]), sb("rstd2", [P, NB])
        power = sb("power", [P, B * NB])
        xn, xnT = sb("xn", [P, B * NB, D]), sb("xnT", [P, B, T])
        rot = sb("rot", [P, 4, T])
        rest = sb("rest", [P, 2, T])
        parts = sb("parts", [P, 2, 3, T], BF16)
        v_nat = sb("v_nat", [P, B, NB, D])
        v_aug = sb("v_aug", [P, NB, H, 32])
        pick = sb("pick", [P, 2, 3, 2, P], BF16)
        m_row = sb("m_row", [P, 2, UH * NB])
        m_rest = sb("m_rest", [P, UH * NB])
        m_parts = sb("m_parts", [P, 3, UH * NB], BF16)
        mT = sb("mT", [3 * UH * NB, P], BF16)
        pT = sb("pT", [P, 2, NS, T])
        o_sb = sb("o_sb", [P, 2, T])
        denom = sb("denom", [P, NB, 8])
        o_nat, oT = sb("o_nat", [P, NB, D]), sb("oT", [P, T])
        x2, xn2, xn2T = sb("x2", [P, NB, D]), sb("xn2", [P, NB, D]), sb("xn2T", [P, T])
        th, gated = sb("th", [P, T]), sb("gated", [P, T])
        hT = sb("hT", [P, NC, T])

        nat_b = [bank(f"nat{n}") for n in range(NAT_BANKS)]
        st_b = [bank(f"st{n}") for n in range(ST_BANKS)]
        o_b = bank("o")
        m_b = [bank("misc0"), bank("misc1")]
        norm_b, on_b, wo_b, x2t_b = (m_b[1], m_b[0]), (nat_b[0], nat_b[1]), (st_b[0], st_b[1]), (st_b[2], o_b)
        gu_b = [(m_b[1], m_b[0], nat_b[0]), (nat_b[1], st_b[0], st_b[1])]
        down_b = x2t_b
        L = B - 1
        pick_b = [(st_b[0], st_b[1]), (st_b[2], o_b)]

        x0_in, x_in, w_in, wi_in = sem("x0_in"), sem("x_in"), sem("w_in"), sem("wi_in")
        c_in, id_in = sem("c_in"), sem("id_in")
        ones_in, scr_q, scr_k = sem("ones_in"), sem("scr_q"), sem("scr_k")
        pair_in = [sem("pair0_in"), sem("pair1_in")]
        m_in = [sem("m_in0"), sem("m_in1")]
        stored = sem("stored")
        nat_done, st_done, pv_done, mt_done = sem("nat_done"), sem("st_done"), sem("pv_done"), sem("mt_done")
        xt_done, proj_done, ot_done, ont_done = sem("xt_done"), sem("proj_done"), sem("ot_done"), sem("ont_done")
        v_done = sem("v_done")
        wo_done, x2t_done, gu_done, down_done = sem("wo_done"), sem("x2t_done"), sem("gu_done"), sem("down_done")
        picked = sem("picked")
        max_done, rot_done, const_done = sem("max_done"), sem("rot_done"), sem("const_done")
        ln1, ln2, xn_done, xn2_done = sem("ln1"), sem("ln2"), sem("xn_done"), sem("xn2_done")
        denom_done, onat_done, x2_done = sem("denom_done"), sem("onat_done"), sem("x2_done")
        gated_done, h_done, y_done = sem("gated_done"), sem("h_done"), sem("y_done")
        dve_in = sem("dve_in")
        act_in, pick_set = sem("act_in"), sem("pick_set")
        exp_done, mtc_done, xtc_done, vc_done = sem("exp_done"), sem("mtc_done"), sem("xtc_done"), sem("vc_done")
        oc_done, ontc_done, x2tc_done, tanh_done = sem("oc_done"), sem("ontc_done"), sem("x2tc_done"), sem("tanh_done")
        clear_done, mp, mask_done = sem("clear_done"), sem("mp"), sem("mask_done")
        split = [sem("split_q"), sem("split_k")]
        va_done, rs1_done, rs2_done = sem("va_done"), sem("rs1_done"), sem("rs2_done")
        MASKS = 5
        CLEARED = 9
        MP, SPLIT = 4, 5

        block = ctx.enter_context(nc.Block())

        @block.tensor
        def _(pe):
            def nat_step(u, g, i):
                j, a0, n = NAT[i]
                w = P * (j + 1)
                out = nat_b[NAT_SEQ[g * NN + i]]
                ago = back(NAT_SEQ, g * NN + i)
                if not (isinstance(u, int) and u * NN + i < ago):
                    pe.wait_ge(max_done, u * NN + i + 1 - ago)
                o3 = out[:, 0:n * w].rearrange("p (a k) -> p a k", a=n)
                pe.matmul(o3[:, :, P * j:w], ident16[:, :],
                          mask16[:, :].unsqueeze(1).broadcast_to([P, n, P]) if n > 1 else mask16[:, :].unsqueeze(1),
                          start=True, stop=False, skip_group_check=True)
                for a in range(n):
                    h = UH * g + a0 + a
                    mm = pe.matmul(o3[:, a, :], qx[:, h, P * j:P * j + P], kx[:, h, 0:w],
                                   start=False, stop=True, skip_group_check=True)
                mm.then_inc(nat_done, 1)

            def st_step(u, b, g, i):
                if i == 0:
                    pe.wait_ge(m_in[g % 2], 16 * (G // 2 * b + g // 2 + 1))
                ago = back(ST_SEQ, g * NS + i)
                if not (isinstance(u, int) and u * NS + i < ago):
                    pe.wait_ge(exp_done, u * NS + i + 1 - ago)
                for a, kb, c in STS[i]:
                    h = UH * g + a
                    mm = pe.matmul(st_b[ST_SEQ[g * NS + i]][:, c:c + T - P * kb], kx[:, h, P * kb:P * kb + P],
                                   qx[:, h, P * kb:T], start=True, stop=True)
                mm.then_inc(st_done, 1)

            def pv_step(u, g, kb, b, first):
                need = {0: 1, 1: 2, 3: 3, 2: 5}[kb]
                pe.wait_ge(mask_done, u * MASKS + need)
                if kb == 0 and g == 0:
                    pe.wait_ge(va_done, b + 1)
                if kb == 0 and g % 2 == 0 and not (first and g == 0):
                    pe.wait_ge(oc_done, 2 * b + g // 2)
                for a in range(UH):
                    n, c = PLACE[a, kb]
                    mm = pe.matmul(o_b[32 * a:32 * a + 32, P * kb:T], v_aug[:, kb, UH * g + a, :],
                                   pT[:, g % 2, n, c:c + T - P * kb],
                                   start=(g % 2 == 0 and kb == 0), stop=(g % 2 == 1 and kb == 2),
                                   skip_group_check=True)
                if kb == 2:
                    mm.then_inc(pv_done, 1)

            def max_T(u):
                n = MP * (u + 1) if isinstance(u, int) else pe.to_reg(MP * (u + 1))
                pe.wait_ge(const_done, 1)
                pe.wait_ge(mp, n)
                pe.transpose(m_b[0][0:3 * UH * NB, 0:P // 2].bitcast(BF16),
                             m_parts[:, :, :].rearrange("p c m -> p (c m)"), ident16[:, :]).then_inc(mt_done, 1)

            def four_T(out, src, done):
                for i in range(NB):
                    mm = pe.transpose(out[:, P * i:P * i + P], src(i), ident[:, :])
                mm.then_inc(done, 1)

            def xn_T(b):
                pe.wait_ge(xn_done, b + 1)
                if b:
                    pe.wait_ge(xtc_done, b)
                four_T(m_b[1], lambda i: xn[:, NB * b + i, :], xt_done)

            def project(b, n):
                pe.matmul(m_b[PROJ_BANK[n]][:, :], w_proj[:, n, :], xnT[:, b, :], start=True,
                          stop=True).then_inc(proj_done, 1)

            def values(b):
                if b:
                    pe.wait_ge(vc_done, b)
                for i in range(NB):
                    mm = pe.matmul(m_b[0][:, P * i:P * i + P], xnT[:, b, P * i:P * i + P], w_proj[:, 4, :],
                                   start=True, stop=True)
                mm.then_inc(v_done, 1)

            def o_T(b, t):
                pe.wait_ge(oc_done, 2 * b + t + 1)
                four_T(m_b[t], lambda i: o_sb[:, t, P * i:P * i + P], ot_done)

            def on_T(b):
                pe.wait_ge(onat_done, 2 * b + 2)
                four_T(m_b[1], lambda i: o_nat[:, i, :], ont_done)

            def w_o(b):
                pe.wait_ge(ontc_done, b + 1)
                for i in range(NB):
                    mm = pe.matmul(m_b[0][:, P * i:P * i + P], oT[:, P * i:P * i + P], w_proj[:, 5, :],
                                   start=True, stop=True)
                mm.then_inc(wo_done, 1)

            def xn2_T(b):
                pe.wait_ge(xn2_done, 2 * b + 2)
                four_T(m_b[1], lambda i: xn2[:, i, :], x2t_done)

            def gate_up(b, c, n):
                pe.matmul(m_b[n][:, :], w_ffn[:, n, P * c:P * c + P], xn2T[:, :],
                          start=True, stop=True).then_inc(gu_done, 1)

            def down(b, i):
                if i == 0:
                    pe.wait_ge(h_done, NC * b + NC)
                for c in range(NC):
                    mm = pe.matmul(m_b[1][:, P * i:P * i + P], hT[:, c, P * i:P * i + P],
                                   w_ffn[:, 2, P * c:P * c + P], start=(c == 0), stop=(c == NC - 1))
                if i == NB - 1:
                    mm.then_inc(down_done, 1)

            def body(b, first, last):
                for g in range(G):
                    u = b * G + g
                    for p in range(POS):
                        if p < NN and not (last and g == G - 1):
                            ng = (g + 1) % G
                            nb_ = b + 1 if g == G - 1 else b
                            if p == 0 and first and g == 0:
                                pe.wait_ge(pair_in[0], 32)
                            if p == 0 and ng % 2 == 0:
                                pe.wait_ge(pair_in[ng // 2], 48 * nb_ + 32)
                            nat_step(u + 1, ng, p)
                        if first and g == 3 and p == 0:
                            pe.wait_ge(const_done, 3)
                        if p == PE_AT["max_T"]:
                            if g == 0 and first:
                                pe.wait_ge(vc_done, 2)
                            if g == 0 and not first:
                                pe.wait_ge(onat_done, 2 * b - 1)
                            if g == 1 and first:
                                pe.wait_ge(rot_done, 4 * (b + 1) + 2)
                            if g == 1 and not first:
                                pe.wait_ge(x2_done, b)
                            if g == 2 and first:
                                pe.wait_ge(rot_done, 4 * (b + 1) + 4)
                            if g == 3 and first:
                                pe.wait_ge(vc_done, B - 1)
                            if g >= 2 and not first:
                                pe.wait_ge(gated_done, NC * (b - 1) + 1 + 2 * (g - 2))
                            max_T(u)
                        if p in PV_AT and not (first and g == 0):
                            pv_step(u - 1, (g - 1) % G, PV_AT[p], b - 1 if g == 0 else b,
                                    first if g else False)
                        if last and g == 3 and p == 12:
                            pv_step(u, g, 0, b, False)
                        if g == 0 and not last:
                            if p == PE_AT["q"]:
                                project(b + 1, 0)
                            if p == PE_AT["q_swap"]:
                                pe.wait_ge(mtc_done, u + 1)
                                project(b + 1, 1)
                        if g == 0 and not first:
                            if p == PE_AT["o_T1"]:
                                if not last:
                                    pe.wait_ge(rot_done, 4 * (b + 1) + 1)
                                o_T(b - 1, 1)
                            if p == PE_AT["on_T"]:
                                on_T(b - 1)
                            if p == PE_AT["w_o"]:
                                if last:
                                    pe.wait_ge(mtc_done, u + 1)
                                else:
                                    pe.wait_ge(rot_done, 4 * (b + 1) + 2)
                                w_o(b - 1)
                        if g == 1 and not last:
                            if p == PE_AT["k"]:
                                project(b + 1, 2)
                            if p == PE_AT["k_swap"]:
                                pe.wait_ge(mtc_done, u + 1)
                                project(b + 1, 3)
                        if g == 1 and not first:
                            if p == PE_AT["xn2_T"]:
                                if not last:
                                    pe.wait_ge(rot_done, 4 * (b + 1) + 3)
                                xn2_T(b - 1)
                            if p == PE_AT["gate0"]:
                                if last:
                                    pe.wait_ge(mtc_done, u + 1)
                                else:
                                    pe.wait_ge(rot_done, 4 * (b + 1) + 4)
                                pe.wait_ge(x2tc_done, b)
                                gate_up(b - 1, 0, 0)
                            if p == PE_AT["up0"]:
                                gate_up(b - 1, 0, 1)
                        if g == 2 and not first:
                            if p == PE_AT["gate1"]:
                                pe.wait_ge(mtc_done, u + 1)
                                gate_up(b - 1, 1, 0)
                            if p == PE_AT["up1"]:
                                pe.wait_ge(h_done, NC * (b - 1) + 1)
                                gate_up(b - 1, 1, 1)
                            if p == PE_AT["gate2"]:
                                pe.wait_ge(gated_done, NC * (b - 1) + 2)
                                gate_up(b - 1, 2, 0)
                            if p == PE_AT["up2"]:
                                pe.wait_ge(h_done, NC * (b - 1) + 2)
                                gate_up(b - 1, 2, 1)
                        if g == 3 and not first:
                            for i in range(NB):
                                if p == PE_AT[f"down{i}"]:
                                    down(b - 1, i)
                        if g >= 2 and first:
                            if p == 4:
                                xn_T(g)
                            if p == 7:
                                pe.wait_ge(mtc_done, u + 1)
                                pe.wait_ge(xtc_done, g + 1)
                                values(g)
                        if g == 3 and p == PE_AT["o_T0"]:
                            if first:
                                pe.wait_ge(vc_done, B)
                            else:
                                pe.wait_ge(mtc_done, u + 1)
                            o_T(b, 0)
                        if p >= ST_AT:
                            st_step(u, b, g, p - ST_AT)

            def keep_warm(n, out):
                for i in range(WARM[n]):
                    pe.matmul(out[:, :], minus[:, 0:P], minus[:, :], start=True, stop=True)

            pe.wait_ge(clear_done, 2)
            keep_warm(0, nat_b[0])
            pe.wait_ge(id_in, 16)
            xn_T(0)
            pe.wait_ge(w_in, 16)
            pe.wait_ge(xtc_done, 1)
            project(0, 0)
            project(0, 1)
            pe.wait_ge(rot_done, 1)
            project(0, 2)
            pe.wait_ge(rot_done, 2)
            project(0, 3)
            pe.wait_ge(rot_done, 4)
            values(0)
            xn_T(1)
            pe.wait_ge(pick_set, 1)
            for w, n in ((0, 0), (1, 0), (0, 1), (0, 2), (1, 1), (1, 2)):
                pe.wait_ge(split[w], min(2 * n + 2, SPLIT))
                for pair in range(2):
                    mm = pe.matmul(pick_b[w][pair][:, :], pick[:, w, n, pair, :], parts[:, w, n, :],
                                   start=(n == 0), stop=(n == 2), skip_group_check=True)
                if n == 2:
                    mm.then_inc(picked, 1)
            pe.wait_ge(const_done, 2)
            pe.wait_ge(ones_in, 32)
            for i in range(NN):
                a = NAT[i][1] + NAT[i][2] - 1
                pe.wait_ge(act_in, a + 1 if a < 2 else a + 3)
                pe.wait_ge(dve_in, min(a, 1) + 1)
                nat_step(0, 0, i)
            pe.wait_ge(xtc_done, 2)
            pe.wait_ge(vc_done, 1)
            values(1)
            body(0, True, False)
            with pe.Fori(1, B - 1) as b:
                body(b, False, False)
            body(B - 1, False, True)
            for kb in (1, 3, 2):
                pv_step(B * G - 1, G - 1, kb, L, False)

            def turn_half(out, src, half, done):
                for i in range(HB):
                    mm = pe.transpose(out[:, P * i:P * i + P], src(HB * half + i), ident[:, :])
                mm.then_inc(done, 1)

            pe.wait_ge(oc_done, 2 * L + 2)
            pe.wait_ge(onat_done, 2 * L + 1)
            for half in range(2):
                turn_half(norm_b[half], lambda i: o_sb[:, 1, P * i:P * i + P], half, ot_done)
            for half in range(2):
                pe.wait_ge(onat_done, 2 * L + 1 + half + 1)
                turn_half(on_b[half], lambda i: o_nat[:, i, :], half, ont_done)
            for half in range(2):
                pe.wait_ge(ontc_done, L + half + 1)
                for i in range(HB):
                    k = P * (HB * half + i)
                    mm = pe.matmul(wo_b[half][:, P * i:P * i + P], oT[:, k:k + P], w_proj[:, 5, :],
                                   start=True, stop=True)
                mm.then_inc(wo_done, 1)
            keep_warm(1, down_b[0])
            for half in range(2):
                if half == 0:
                    pe.wait_ge(xn2_done, 2 * L + 1)
                    turn_half(x2t_b[0], lambda i: xn2[:, i, :], 0, x2t_done)
                pe.wait_ge(x2tc_done, L + half + 1)
                for c in range(NC):
                    if half == 0 and c == NC - 1:
                        pe.wait_ge(xn2_done, 2 * L + 2)
                        turn_half(x2t_b[1], lambda i: xn2[:, i, :], 1, x2t_done)
                    for n in range(2):
                        pe.matmul(gu_b[half][c][:, HT * n:HT * n + HT], w_ffn[:, n, P * c:P * c + P],
                                  xn2T[:, HT * half:HT * half + HT], start=True, stop=True).then_inc(gu_done, 1)
            for half in range(2):
                pe.wait_ge(h_done, NC * (L + half + 1))
                for i in range(HB):
                    k = P * (HB * half + i)
                    for c in range(NC):
                        mm = pe.matmul(down_b[half][:, P * i:P * i + P], hT[:, c, k:k + P],
                                       w_ffn[:, 2, P * c:P * c + P], start=(c == 0), stop=(c == NC - 1))
                mm.then_inc(down_done, 1)

        @block.vector
        def _(dve):
            def row_max(u, g, i):
                j, a0, n = NAT[i]
                w = P * (j + 1)
                dve.wait_ge(nat_done, u * NN + i + 1)
                if i == 0 and not (isinstance(u, int) and u < 2):
                    dve.wait_ge(mp, MP * (u - 1))
                dve.reduce_max(m_row[:, g % 2, NB * a0 + j:NB * (a0 + n - 1) + j + 1:NB],
                               nat_b[NAT_SEQ[g * NN + i]][:, 0:n * w].rearrange("p (a k) -> p a k", a=n),
                               AX.X).then_inc(max_done, 1)

            def spread(src, st, step, tiles=NB):
                for i in range(tiles):
                    last = dve.bn_stats(st(i), src(i))
                last.then_inc(step, 1)

            def means(n, st, mv, step, tiles=NB):
                n = n if isinstance(n, int) else dve.to_reg(n)
                dve.wait_ge(x0_in, 16)
                dve.wait_ge(step, n)
                for i in range(tiles):
                    last = dve.bn_aggr(mv(i), st(i))
                last.then_inc(step, 1)

            def centre(dst, src, mv, rs, done, tiles=NB):
                for i in range(tiles):
                    last = dve.tensor_scalar(dst(i), src(i), mv(i)[:, 0:1], rs(i), ALU.subtract, ALU.mult)
                last.then_inc(done, 1)

            def spread1(i0, tiles, turn):
                spread(lambda i: x_sb[:, i0 + i, :], lambda i: stats[:, i0 + i, :], ln1, tiles)

            def means1(i0, tiles, turn):
                means(2 * turn + 1, lambda i: stats[:, i0 + i, :], lambda i: mean_var[:, i0 + i, :], ln1, tiles)

            def centre1(b):
                dve.wait_ge(rs1_done, min(2 * b + 2, 6))
                centre(lambda i: xn[:, NB * b + i, :], lambda i: x_sb[:, NB * b + i, :],
                       lambda i: mean_var[:, NB * b + i, :], lambda i: rstd[:, NB * b + i:NB * b + i + 1], xn_done)

            def spread2(b):
                dve.wait_ge(x2_done, b + 1)
                spread(lambda i: x2[:, i, :], lambda i: stats2[:, i, :], ln2)

            def means2(b):
                means(2 * b + 1, lambda i: stats2[:, i, :], lambda i: mean_var2[:, i, :], ln2)

            def centre2(b, half):
                dve.wait_ge(rs2_done, 2 * b + 2)
                k = NB // 2 * half
                centre(lambda i: xn2[:, k + i, :], lambda i: x2[:, k + i, :], lambda i: mean_var2[:, k + i, :],
                       lambda i: rstd2[:, k + i:k + i + 1], xn2_done, NB // 2)

            def rotate(b, n):
                dve.wait_ge(proj_done, 4 * b + n + 1)
                if n % 2 == 0 and not (isinstance(b, int) and b == 0):
                    dve.wait_ge(split[n // 2], SPLIT * (b - 1) + 1)
                dve.tensor_tensor(rot[:, n, :], m_b[PROJ_BANK[n]][:, :], cos if n % 2 == 0 else sin,
                                  ALU.mult).then_inc(rot_done, 1)

            def normalise(b, t):
                dve.wait_ge(ot_done, 2 * b + t + 1)
                o4 = m_b[t][:, :].rearrange("p (i a s e) -> p i a s e", i=NB, a=UH, s=2)
                dn = denom[:, :, :].rearrange("p i (a s) -> p i a s", s=2)
                dve.reciprocal(dn, o4[:, :, :, :, DH]).then_inc(denom_done, 1)
                dve.wait_ge(denom_done, 2 * b + t + 1)
                on = o_nat[:, :, :].rearrange("p i (t s a e) -> p i t s a e", t=2, s=2, a=UH)
                for s in range(2):
                    last = dve.tensor_tensor(on[:, :, t, s, :, :], o4[:, :, :, s, 0:DH],
                                             dn[:, :, :, s].unsqueeze(3).broadcast_to([P, NB, UH, DH]), ALU.mult)
                last.then_inc(onat_done, 1)

            def add_x(b):
                dve.wait_ge(wo_done, b + 1)
                xs = x_sb[:, :, :].rearrange("p (b n) d -> p b (n d)", b=B)
                dve.tensor_tensor(x2[:, :, :].rearrange("p i d -> p (i d)"), m_b[0][:, :], xs[:, b, :],
                                  ALU.add).then_inc(x2_done, 1)

            def hidden_gate(b, c):
                dve.wait_ge(tanh_done, NC * b + c + 1)
                dve.scalar_tensor_tensor(gated[:, :], th[:, :], 1.0, m_b[0][:, :], ALU.add,
                                         ALU.mult).then_inc(gated_done, 1)

            def hidden_up(b, c):
                dve.wait_ge(gated_done, NC * b + c + 1)
                dve.wait_ge(gu_done, 2 * (NC * b + c) + 2)
                dve.scalar_tensor_tensor(hT[:, c, :], gated[:, :], 0.5, m_b[1][:, :], ALU.mult,
                                         ALU.mult).then_inc(h_done, 1)

            def add_y(b):
                dve.wait_ge(down_done, b + 1)
                x2f = x2[:, :, :].rearrange("p i d -> p (i d)")
                dve.tensor_tensor(x2f, m_b[1][:, :], x2f, ALU.add).then_inc(y_done, 1)

            def body(b, first, last):
                for g in range(G):
                    u = b * G + g
                    for p in range(POS):
                        if p < NN and not (last and g == G - 1):
                            row_max(u + 1, (g + 1) % G, p)
                        if first and g == 0 and p == 12:
                            spread1(2 * NB, 2 * NB, 2)
                        if first and g == 0 and p == 13:
                            means1(2 * NB, 2 * NB, 2)
                        if first and g in (1, 2) and p == 12:
                            centre1(g + 1)
                        if first and g == 1 and p == 13:
                            dve.wait_ge(wi_in, 16)
                            dve.tensor_scalar(w_ffn[:, :, :], w_int[:, :, :], W_SCALE, None,
                                              ALU.mult).then_inc(const_done, 1)
                        for n in range(2):
                            if g < 2 and not last and p == DVE_AT["qk"[g] + ("", "_swap")[n]]:
                                rotate(b + 1, 2 * g + n)
                        if g == 0 and not first:
                            if p == DVE_AT["norm1"]:
                                normalise(b - 1, 1)
                            if p == DVE_AT["add_x"]:
                                add_x(b - 1)
                            if p == DVE_AT["spread"]:
                                spread2(b - 1)
                        if g == 1 and not first:
                            if p == DVE_AT["means"]:
                                means2(b - 1)
                            for half in range(2):
                                if p == DVE_AT[f"centre{half}"]:
                                    centre2(b - 1, half)
                        for c in range(NC):
                            if g == (1, 2, 2)[c] and not first:
                                if p == DVE_AT[f"gate{c}"]:
                                    hidden_gate(b - 1, c)
                                if p == DVE_AT[f"up{c}"]:
                                    hidden_up(b - 1, c)
                        if g == 3 and p == DVE_AT["add_y"] and not first:
                            add_y(b - 1)
                        if g == 3 and p == DVE_AT["norm0"]:
                            normalise(b, 0)

            def rotated(w):
                dve.wait_ge(rot_done, 2 * w + 2)
                dve.tensor_tensor(rest[:, w, :], rot[:, 2 * w, :], rot[:, 2 * w + 1, :], ALU.add).then_inc(split[w], 1)

            def left(n):
                dve.wait_ge(split[1], 2 * n + 2)
                dve.tensor_tensor(parts[:, 1, 2, :] if n else rest[:, 1, :], rest[:, 1, :], parts[:, 1, n, :],
                                  ALU.subtract).then_inc(split[1], 1)

            dve.wait_ge(x0_in, 16)
            spread1(0, NB, 0)
            means1(0, NB, 0)
            centre1(0)
            dve.wait_ge(id_in, 16)
            dve.wait_ge(c_in, 16)
            dve.tensor_copy(ident16[:, :], ident[:, :]).then_inc(const_done, 1)
            dve.tensor_copy(mask16[:, :], mask).then_inc(const_done, 1)
            dve.wait_ge(x_in, 16)
            spread1(NB, NB, 1)
            means1(NB, NB, 1)
            rotate(0, 0)
            rotate(0, 1)
            rotated(0)
            rotate(0, 2)
            rotate(0, 3)
            rotated(1)
            centre1(1)
            left(0)
            left(1)
            dve.wait_ge(picked, 2)
            dve.wait_ge(clear_done, 6)
            for s in range(2):
                dve.tensor_copy(kx[0:XR, s, :], pick_b[1][0][64 * s:64 * s + XR, :]).then_inc(dve_in, 1)
            for i in range(NN):
                row_max(0, 0, i)
            body(0, True, False)
            with dve.Fori(1, B - 1) as b:
                body(b, False, False)
            body(B - 1, False, True)

            def half_of(t, half):
                return t[:, HT * half:HT * half + HT]

            def blocks(half):
                return slice(HB * half, HB * half + HB)

            for half in range(2):
                n = 2 * L + 1 + half + 1
                dve.wait_ge(ot_done, n)
                o4 = norm_b[half][:, 0:HT].rearrange("p (i a s e) -> p i a s e", i=HB, a=UH, s=2)
                dn = denom[:, blocks(half), :].rearrange("p i (a s) -> p i a s", s=2)
                dve.reciprocal(dn, o4[:, :, :, :, DH]).then_inc(denom_done, 1)
                dve.wait_ge(denom_done, n)
                on = o_nat[:, blocks(half), :].rearrange("p i (t s a e) -> p i t s a e", t=2, s=2, a=UH)
                for s in range(2):
                    mul = dve.tensor_tensor(on[:, :, 1, s, :, :], o4[:, :, :, s, 0:DH],
                                            dn[:, :, :, s].unsqueeze(3).broadcast_to([P, HB, UH, DH]), ALU.mult)
                mul.then_inc(onat_done, 1)
            dve.wait_ge(stored, 16 * L)
            for half in range(2):
                k = HB * half
                dve.wait_ge(wo_done, L + half + 1)
                dve.tensor_tensor(x2[:, blocks(half), :].rearrange("p i d -> p (i d)"), wo_b[half][:, 0:HT],
                                  x_sb[:, NB * L + k:NB * L + k + HB, :].rearrange("p i d -> p (i d)"),
                                  ALU.add).then_inc(x2_done, 1)
                dve.wait_ge(x2_done, L + half + 1)
                spread(lambda i: x2[:, k + i, :], lambda i: stats2[:, k + i, :], ln2, HB)
                means(2 * (L + half) + 1, lambda i: stats2[:, k + i, :], lambda i: mean_var2[:, k + i, :], ln2, HB)
            for half in range(2):
                dve.wait_ge(rs2_done, 2 * (L + half) + 2)
                k = HB * half
                centre(lambda i: xn2[:, k + i, :], lambda i: x2[:, k + i, :], lambda i: mean_var2[:, k + i, :],
                       lambda i: rstd2[:, k + i:k + i + 1], xn2_done, HB)
            for half in range(2):
                for c in range(NC):
                    n = NC * (L + half) + c + 1
                    th_h, gu = half_of(rot[:, c, :], half), gu_b[half][c]
                    dve.wait_ge(tanh_done, n)
                    dve.scalar_tensor_tensor(th_h, th_h, 1.0, gu[:, 0:HT], ALU.add,
                                             ALU.mult).then_inc(gated_done, 1)
                    dve.wait_ge(gated_done, n)
                    dve.scalar_tensor_tensor(half_of(hT[:, c, :], half), th_h, 0.5, gu[:, HT:T], ALU.mult,
                                             ALU.mult).then_inc(h_done, 1)
            for half in range(2):
                dve.wait_ge(down_done, L + half + 1)
                y = x2[:, blocks(half), :].rearrange("p i d -> p (i d)")
                dve.tensor_tensor(y, down_b[half][:, 0:HT], y, ALU.add).then_inc(y_done, 1)

        @block.scalar
        def _(act):
            def exp_step(u, g, i):
                act.wait_ge(st_done, u * NS + i + 1)
                if i == 0 and not (isinstance(u, int) and u < 2):
                    act.wait_ge(pv_done, u - 1)
                w = 512
                act.activation(pT[:, g % 2, i, 0:w], st_b[ST_SEQ[g * NS + i]][:, 0:w], ACT.Exp, scale=SCALE).then_inc(exp_done, 1)

            def copy_out(dst, src, wait, n, done):
                act.wait_ge(wait, n)
                act.activation(dst, src, ACT.Copy).then_inc(done, 1)

            def max_rows(u, b, g):
                if not (isinstance(u, int) and u == 0):
                    act.wait_ge(m_in[(g - 1) % 2], 16 * (G // 2 * b + (g + 1) // 2))
                copy_out(mT[:, :], m_b[0][0:3 * UH * NB, 0:P // 2].bitcast(BF16), mt_done, u + 1, mtc_done)

            def xn_T(b):
                copy_out(xnT[:, b, :], m_b[1][:, :], xt_done, b + 1, xtc_done)

            def v_copy(b):
                copy_out(v_nat[:, b, :, :].rearrange("p i d -> p (i d)"), m_b[0][:, :], v_done, b + 1, vc_done)

            def cast(b, w, n):
                done = split[w]
                act.wait_ge(done, SPLIT * b + 2 * n + 1)
                if n == 0 and not (isinstance(b, int) and b == 0):
                    act.wait_ge((scr_q, scr_k)[w], 16 * len(RUNS) * (b + 1))
                act.activation(parts[:, w, n, :], rest[:, w, :], ACT.Copy).then_inc(done, 1)

            def lay_values(b, first):
                act.wait_ge(vc_done, 1 if first else B)
                if first:
                    act.wait_ge(clear_done, CLEARED)
                else:
                    act.wait_ge(pv_done, G * b)
                va = v_aug[:, :, :, :].rearrange("p k (t s a) e -> p (k t) s a e", t=2, s=2)
                vn = v_nat[:, :, :, :].rearrange("p b k (t s a e) -> p b (k t) s a e", t=2, s=2, a=UH)
                for s in range(2):
                    last = act.activation(va[:, :, s, :, 16 * s:16 * s + DH], vn[:, b, :, s, :, :], ACT.Copy)
                last.then_inc(va_done, 1)

            def o_copy(b, t):
                copy_out(o_sb[:, t, :], o_b[:, :], pv_done, G * b + 2 * t + 2, oc_done)

            def on_T(b):
                copy_out(oT[:, :], m_b[1][:, :], ont_done, b + 1, ontc_done)

            def xn2_T(b):
                copy_out(xn2T[:, :], m_b[1][:, :], x2t_done, b + 1, x2tc_done)

            def tanh(b, c):
                act.wait_ge(gu_done, 2 * (NC * b + c) + 1)
                act.activation(th[:, :], m_b[0][:, :], ACT.Tanh, scale=0.5).then_inc(tanh_done, 1)

            def body(b, first, last):
                for g in range(G):
                    u = b * G + g
                    for p in range(POS):
                        if p == ACT_AT["max"]:
                            max_rows(u, b, g)
                        if g == 0 and p == ACT_AT["values"]:
                            lay_values(b, first)
                        if g == 0 and not first and p == ACT_AT["o_copy1"]:
                            o_copy(b - 1, 1)
                        if g < 2 and not last and p == ACT_AT["qk"[g] + "0"]:
                            cast(b + 1, g, 0)
                        if g == 0 and not first and p == ACT_AT["on_T"]:
                            on_T(b - 1)
                        if g == 1 and not first and p == ACT_AT["xn2_T"]:
                            xn2_T(b - 1)
                        for c in range(NC):
                            if g == (1, 2, 2)[c] and not first and p == ACT_AT[f"tanh{c}"]:
                                tanh(b - 1, c)
                        if g < 2 and not last and p == ACT_AT["qk"[g] + "1"]:
                            cast(b + 1, g, 1)
                        if g == 2 and p == ACT_AT["o_copy0"]:
                            o_copy(b, 0)
                        if g >= 2 and first and p == 5:
                            xn_T(g)
                        if g >= 2 and first and p == 8:
                            v_copy(g)
                        if p >= ST_AT:
                            exp_step(u, g, p - ST_AT)

            act.wait_ge(id_in, 16)
            act.wait_ge(clear_done, 4)
            terms = [(m, part) for n, part in RUNS for m in range(n)]
            heads_i = ident[:, 0:UH * DH].rearrange("p (a s i) -> p a s i", a=2, s=2)
            for t, both in enumerate(terms):
                for w in range(2):
                    to = pick[:, w, both[w], :, :].rearrange("p a (s c) -> p a s c", s=2)
                    last = act.activation(to[:, :, :, DH * t:DH * t + DH], heads_i, ACT.Copy)
            last.then_inc(pick_set, 1)

            def row_copy(w, a):
                act.activation((qx, kx)[w][0:XR, a, :], pick_b[w][a // 2][64 * (a % 2):64 * (a % 2) + XR, :],
                               ACT.Copy).then_inc(act_in, 1)

            xn_T(0)
            for w in range(2):
                for n in range(2):
                    cast(0, w, n)
            act.wait_ge(clear_done, 7)
            act.wait_ge(picked, 1)
            for a in range(UH):
                row_copy(0, a)
            act.wait_ge(picked, 2)
            for a in range(2, UH):
                row_copy(1, a)
            v_copy(0)
            xn_T(1)
            v_copy(1)
            body(0, True, False)
            with act.Fori(1, B - 1) as b:
                body(b, False, False)
            body(B - 1, False, True)

            def half_of(t, half):
                return t[:, HT * half:HT * half + HT]

            o_copy(L, 1)
            for half in range(2):
                copy_out(half_of(oT, half), on_b[half][:, 0:HT], ont_done, L + half + 1, ontc_done)
            copy_out(half_of(xn2T, 0), x2t_b[0][:, 0:HT], x2t_done, L + 1, x2tc_done)
            for half in range(2):
                for c in range(NC):
                    if half == 0 and c == NC - 1:
                        copy_out(half_of(xn2T, 1), x2t_b[1][:, 0:HT], x2t_done, L + 2, x2tc_done)
                    n = NC * (L + half) + c + 1
                    act.wait_ge(gu_done, 2 * n)
                    act.activation(half_of(rot[:, c, :], half), gu_b[half][c][:, 0:HT], ACT.Tanh,
                                   scale=0.5).then_inc(tanh_done, 1)

        @block.gpsimd
        def _(pool):
            def wait(signal, n):
                if not isinstance(n, int):
                    n = pool.to_reg(n)
                    pool.wait_ge(clear_done, 1)
                pool.wait_ge(signal, n)

            def split_max(u, g):
                wait(max_done, NN * (u + 1))
                if not (isinstance(u, int) and u == 0):
                    wait(mt_done, u)
                pool.tensor_copy(m_parts[:, 0, :], m_row[:, g % 2, :]).then_inc(mp, 1)
                wait(mp, MP * u + 1)
                pool.tensor_tensor(m_rest[:, :], m_row[:, g % 2, :], m_parts[:, 0, :], ALU.subtract).then_inc(mp, 1)
                wait(mp, MP * u + 2)
                pool.tensor_copy(m_parts[:, 1, :], m_rest[:, :]).then_inc(mp, 1)
                wait(mp, MP * u + 3)
                pool.tensor_tensor(m_parts[:, 2, :], m_rest[:, :], m_parts[:, 1, :], ALU.subtract).then_inc(mp, 1)

            def causal(u, g, n):
                lo, hi, cols, need = [(0, 4, [0], 4), (4, 8, [0, 384], 8), (8, 10, [0, 256], 10)][n]
                wait(exp_done, NS * u + need)
                for c in cols:
                    v = pT[:, g % 2, lo:hi, c:c + P]
                    pool.affine_select(out=v, in_=v, compare_op=ALU.is_ge, fill=0.0, base=0,
                                       pattern=[[0, hi - lo], [1, P]], channel_multiplier=-1).then_inc(mask_done, 1)

            def split_rot(b, w, stage):
                q, p3, done, n = rest[:, w, :], parts[:, w], split[w], SPLIT * b
                if stage == 0:
                    wait(rot_done, 4 * b + 2 * w + 2)
                    if not (isinstance(b, int) and b == 0):
                        wait(done, n)
                    pool.tensor_tensor(q, rot[:, 2 * w, :], rot[:, 2 * w + 1, :], ALU.add).then_inc(done, 1)
                if stage == 1:
                    wait(done, n + 2)
                    pool.tensor_tensor(q, q, p3[:, 0, :], ALU.subtract).then_inc(done, 1)
                if stage == 2:
                    wait(done, n + 4)
                    pool.tensor_tensor(p3[:, 2, :], q, p3[:, 1, :], ALU.subtract).then_inc(done, 1)

            def root(n, mv, rs, step, done):
                wait(step, n + 2)
                pool.tensor_scalar(rs, mv, EPS, None, ALU.add).then_inc(done, 1)
                wait(done, n + 1)
                pool.tensor_tensor(rs, rs, power[:, 0:rs.shape[1]], ALU.pow).then_inc(done, 1)

            def root2(b):
                root(2 * b, mean_var2[:, :, 1], rstd2[:, :], ln2, rs2_done)

            def body(b, first, last):
                for g in range(G):
                    u = b * G + g
                    if first and g == 1:
                        root(4, mean_var[:, 2 * NB:B * NB, 1], rstd[:, 2 * NB:B * NB], ln1, rs1_done)
                    for job in POOL_ORDER:
                        if job == "root2" and g == 1 and not first:
                            root2(b - 1)
                        if job.startswith("part") and g < 2 and not last:
                            split_rot(b + 1, g, int(job[-1]))
                        if job.startswith("causal"):
                            causal(u, g, int(job[-1]))
                        if job == "max" and not (last and g == G - 1):
                            split_max(u + 1, (g + 1) % G)

            def clear(t, value=0.0):
                pool.memset(t, value).then_inc(clear_done, 1)

            clear(power[:, :], -0.5)
            clear(minus[:, :], -1.0)
            clear(zeros[:, :])
            clear(pick[:, :, :, :, :].rearrange("p w n a c -> p (w n a c)").bitcast(F32))
            kf = kx[:, :, :].rearrange("p h t -> p (h t)").bitcast(F32)
            clear(kf[:, 0:H * T // 4])
            pool.wait_ge(clear_done, 1)
            root(0, mean_var[:, 0:NB, 1], rstd[:, 0:NB], ln1, rs1_done)
            clear(kf[:, H * T // 4:H * T // 2])
            clear(qx[:, :, :].rearrange("p h t -> p (h t)").bitcast(F32))
            root(2, mean_var[:, NB:2 * NB, 1], rstd[:, NB:2 * NB], ln1, rs1_done)
            for n in range(2):
                wait(split[0], 2 * n + 2)
                pool.tensor_tensor(parts[:, 0, 2, :] if n else rest[:, 0, :], rest[:, 0, :], parts[:, 0, n, :],
                                   ALU.subtract).then_inc(split[0], 1)
            clear(v_aug[:, :, :, :])
            pool.wait_ge(clear_done, CLEARED - 1)
            va = v_aug[:, :, :, :].rearrange("p k (t s a) e -> p (k t) s a e", t=2, s=2)
            for s in range(2):
                last = pool.memset(va[:, :, s, :, 16 * s + DH:16 * s + DH + 1], 1.0)
            last.then_inc(clear_done, 1)
            split_max(0, 0)
            body(0, True, False)
            with pool.Fori(1, B - 1) as b:
                body(b, False, False)
            body(B - 1, False, True)
            for half in range(2):
                k = slice(HB * half, HB * half + HB)
                root(2 * (L + half), mean_var2[:, k, 1], rstd2[:, k], ln2, rs2_done)

        @block.sync
        def _(sp):
            def store_run(b, w, run, rows=slice(0, D)):
                n, part = RUNS[run]
                t = sum(m for m, _ in RUNS[:run])
                src = (parts[rows, w, part:part + 1, :].broadcast_to([rows.stop - rows.start, n, T]) if w
                       else parts[rows, w, 0:n, :])
                sp.dma_start((q_scr, k_scr)[w][b, rows, t:t + n, :], src).then_inc((scr_q, scr_k)[w], 16)

            def scratch(b, w):
                sp.wait_ge(split[w], SPLIT * (b + 1))
                for run in range(len(RUNS)):
                    store_run(b, w, run)

            def load_pair(b, t):
                if isinstance(b, int) and b == 0:
                    n = 16 * len(RUNS) * (t + 1)
                else:
                    n = 16 * len(RUNS) * (b + 2)
                    sp.wait_ge(st_done, NS * (G * (b - 1) + 2 * t + 2))
                    sp.dma_start(qx[XR:XR + MR, 8 * t:8 * t + 8, :], zeros[0:24, :]).then_inc(pair_in[t], 16)
                for dst, scr, done in ((qx, q_scr, scr_q), (kx, k_scr, scr_k)):
                    sp.wait_ge(done, n)
                    h0 = UH if isinstance(b, int) and b + t == 0 else 8 * t
                    sp.dma_start(dst[0:XR, h0:8 * t + 8, :],
                                 scr[b, DH * h0:64 * t + 64].rearrange("(h i) t c -> (i t) h c", i=DH)
                                 ).then_inc(pair_in[t], 16)

            def max_rows(u, g):
                sp.wait_ge(mtc_done, u + 1)
                sp.dma_start(qx[XR:XR + MR, UH * g:UH * g + UH, :], mT[:, :]).then_inc(m_in[g % 2], 16)

            def store(b):
                sp.wait_ge(y_done, b + 1)
                sp.dma_start(out_v[b], x2[:, :, :]).then_inc(stored, 16)
                n = 16 * (b + 1) if isinstance(b, int) else sp.to_reg(16 * (b + 1))
                sp.wait_ge(c_in, 16)
                sp.wait_ge(stored, n)

            def body(b, first, last):
                for g in range(G):
                    max_rows(b * G + g, g)
                    if g == 0 and not first:
                        load_pair(b, 1)
                    if g == 1 and not last:
                        scratch(b + 1, 0)
                    if g == 2 and not last:
                        scratch(b + 1, 1)
                        load_pair(b + 1, 0)
                    if g == 3 and not first:
                        store(b - 1)

            sp.dma_start(x_sb[:, 0:NB, :], x_v[0]).then_inc(x0_in, 16)
            sp.dma_start(ident[:, :], ident_d).then_inc(id_in, 16)
            sp.dma_start(w_proj[:, :, :], w_proj_d).then_inc(w_in, 16)
            sp.dma_start(const[:, :], const_d).then_inc(c_in, 16)
            sp.dma_start(x_sb[:, NB:B * NB, :].rearrange("p (b i) d -> p b i d", b=B - 1),
                         X_d[1:B].rearrange("b (i p) d -> p b i d", p=P)).then_inc(x_in, 16)
            sp.dma_start(w_int[:, :, :], w_ffn_d).then_inc(wi_in, 16)
            sp.wait_ge(clear_done, 6)
            sp.dma_start(kx[XR:XR + MR, 0:8, :], minus[0:24, :]).then_inc(ones_in, 16)
            sp.dma_start(kx[XR:XR + MR, 8:16, :], minus[0:24, :]).then_inc(ones_in, 16)
            for t in range(2):
                rows = slice(32 + 32 * t, 64 + 64 * t)
                sp.wait_ge(split[1], 2)
                store_run(0, 1, 0, rows)
                sp.wait_ge(split[0], SPLIT)
                for run in range(len(RUNS)):
                    store_run(0, 0, run, rows)
                sp.wait_ge(split[1], 4)
                store_run(0, 1, 1, rows)
                sp.wait_ge(split[1], SPLIT)
                store_run(0, 1, 2, rows)
                sp.wait_ge(clear_done, 7)
                load_pair(0, t)
            body(0, True, False)
            with sp.Fori(1, B - 1) as b:
                body(b, False, False)
            body(B - 1, False, True)
            for half in range(2):
                k = slice(HB * half, HB * half + HB)
                sp.wait_ge(y_done, L + half + 1)
                sp.dma_start(out_v[L, :, k, :], x2[:, k, :]).then_inc(stored, 16)
            sp.wait_ge(stored, 16 * (L + 2))


def kernel(**inputs):
    import numpy as np
    import concourse.bacc as bacc
    from concourse import mybir as mb
    from concourse.bass_utils import run_bass_kernel_spmd as run

    def turned(name, order=None):
        w = np.asarray(inputs[name])
        return np.ascontiguousarray((w if order is None else w[order]).T)

    swap = np.arange(D) ^ 1
    q, k = "L0_attn_W_q", "L0_attn_W_k"
    proj = [turned(q), turned(q, swap), turned(k), turned(k, swap), turned("L0_attn_W_v"), turned("L0_attn_W_o")]
    down = turned("L0_ffn_w_down").reshape(NC, P, D).transpose(1, 0, 2).reshape(P, HID)
    theta = np.float32(10000.0) ** (np.float32(-2.0) * np.arange(DH // 2, dtype=np.float32) / np.float32(DH))
    angle = np.arange(T, dtype=np.float32)[None, :] * theta.astype(np.float32)[:, None]
    row = (np.arange(D) % DH) // 2
    sign = np.where(np.arange(D) % 2 == 0, -1.0, 1.0).astype(np.float32)[:, None]
    cos, sin = np.cos(angle)[row].astype(np.float32), (np.sin(angle)[row] * sign).astype(np.float32)
    arrays = {
        "x": np.ascontiguousarray(inputs["L0_attn_X"]),
        "w_proj": np.ascontiguousarray(np.stack(proj, axis=1)),
        "w_ffn": np.ascontiguousarray(np.stack([turned("L0_ffn_w_gate"), turned("L0_ffn_w_up"), down], axis=1)),
        "ident": np.eye(P, dtype=np.float32),
        "const": np.concatenate([cos, sin, np.triu(np.full((P, P), MASKED, np.float32), 1)], axis=1),
    }

    nc = bacc.Bacc("TRN2", target_bir_lowering=False, num_devices=1)
    args = [nc.dram_tensor(f"in_{n}", a.shape, mb.dt.from_np(a.dtype), kind="ExternalInput").ap()
            for n, a in arrays.items()]
    args.append(nc.dram_tensor("out_0", (B, T, D), mb.dt.float32, kind="ExternalOutput").ap())
    layer_kernel(nc, *args)
    r = run(nc, [{f"in_{n}": a for n, a in arrays.items()}], core_ids=[0])
    return r.results[0]["out_0"]
```
